# Optimizing a Trainium2 kernel written in Bass

```python
import numpy as np
import jax
import jax.numpy as jnp

def _softmax(x, axis=-1):
    return jax.nn.softmax(x, axis=axis)

def _gelu(x):
    return jax.nn.gelu(x, approximate=True)

def _silu(x):
    return jax.nn.silu(x)

def _sigmoid(x):
    return jax.nn.sigmoid(x)

def _layernorm(x, axis=-1, eps=1e-05):
    m = jnp.mean(x, axis=axis, keepdims=True)
    v = jnp.var(x, axis=axis, keepdims=True)
    return (x - m) / jnp.sqrt(v + eps)

def _scatter_add(tgt, idx, src, axis=0):
    return tgt.at[idx].add(src)

def _segment_sum(src, seg, n):
    return jax.ops.segment_sum(src, seg, n)
kernel_name = 'mk_audio_tower_d1_tok_audfeat256_r4_8ae835'

def setup_inputs(seed: int=0):
    np.random.seed(seed)
    _w = jnp.asarray

    def _rec_inputs():
        import jax
        import jax.numpy as jnp
        _rk = jax.random.key(seed)
        x = -7.10856e-05 + 0.999911 * jax.random.normal(jax.random.fold_in(_rk, 1), (64, 64, 256), jnp.float32)
        return x
    x = _rec_inputs()

    def _L0_tok_setup():
        import jax, jax.numpy as jnp
        import numpy as np
        KERNEL_SIZE = 8
        key = jax.random.key(seed)
        k1, k2 = jax.random.split(key)
        B, F, T = (16, 64, 4096)
        x = jax.random.normal(k1, (B, F, T), dtype=jnp.float32)
        w = jax.random.normal(k2, (1, F), dtype=jnp.float32) * 0.05
        b = jnp.zeros((1,), dtype=jnp.float32)
        return {'x': x, 'w': w, 'b': b}
    _L0_tok_all = _L0_tok_setup()
    _L0_tok_in = {k: v for k, v in _L0_tok_all.items() if k in ('w', 'b')}
    del _L0_tok_all

    def _L0_attn_setup():
        import jax, jax.numpy as jnp
        import numpy as np
        import math
        B, T, D_MODEL = (1, 512, 64)
        N_Q, N_KV = (16, 1)
        D_HEAD = D_MODEL // N_KV
        QPG = N_Q // N_KV
        ROPE_BASE = 10000.0
        WINDOW = 128
        EPS = 1.1920929e-07
        NEG = -1e+30

        def _rope(x, base=ROPE_BASE):
            t, d = (x.shape[-2], x.shape[-1])
            freqs = base ** (-2.0 * jnp.arange(d // 2, dtype=jnp.float32) / d)
            theta = jnp.arange(t, dtype=jnp.float32)[:, None] * freqs[None, :]
            cos, sin = (jnp.cos(theta), jnp.sin(theta))
            x1, x2 = (x[..., 0::2], x[..., 1::2])
            r1 = x1 * cos - x2 * sin
            r2 = x1 * sin + x2 * cos
            return jnp.stack([r1, r2], axis=-1).reshape(x.shape)

        def _rmsnorm(x, w):
            return x * jax.lax.rsqrt(jnp.mean(x * x, axis=-1, keepdims=True) + EPS) * w
        key = jax.random.key(seed)
        k0, k1, k2, k3 = jax.random.split(key, 4)
        x = jax.random.normal(k0, (B, T, D_MODEL), dtype=jnp.float32)
        wq = jax.random.normal(k1, (QPG * N_KV * D_HEAD, D_MODEL), dtype=jnp.float32) * 0.02
        wkv = jax.random.normal(k2, (2 * D_HEAD * N_KV, D_MODEL), dtype=jnp.float32) * 0.02
        wo = jax.random.normal(k3, (D_MODEL, D_HEAD * N_Q * N_KV), dtype=jnp.float32) * 0.02
        q_norm_w = jnp.ones((D_HEAD,), dtype=jnp.float32)
        k_norm_w = jnp.ones((D_HEAD,), dtype=jnp.float32)
        return {'x': x, 'wq': wq, 'wkv': wkv, 'wo': wo, 'q_norm_w': q_norm_w, 'k_norm_w': k_norm_w}
    _L0_attn_all = _L0_attn_setup()
    _L0_attn_in = {k: v for k, v in _L0_attn_all.items() if k in ('wq', 'wkv', 'wo', 'q_norm_w', 'k_norm_w')}
    del _L0_attn_all

    def _L0_ffn_setup():
        import jax, jax.numpy as jnp
        import numpy as np
        NUM_EXPERTS = 8
        TOP_K = 2
        B, S, D = (8, 2048, 64)

        def _moe(tokens, router_w, w1, b1, w2, b2):
            N = tokens.shape[0]
            E = router_w.shape[0]
            logits = tokens.astype(jnp.float32) @ router_w.astype(jnp.float32).T
            probs = jax.nn.softmax(logits, axis=-1)
            rw, re = jax.lax.top_k(probs, TOP_K)
            if TOP_K > 1:
                rw = rw / jnp.maximum(rw.sum(-1, keepdims=True), 1e-12)
            rw = rw.astype(tokens.dtype)
            combine = jnp.zeros((N, E), tokens.dtype).at[jnp.arange(N)[:, None], re].set(rw)
            out = tokens
            for e in range(E):
                h = jax.nn.gelu(tokens @ w1[e] + b1[e], approximate=False)
                y = h @ w2[e] + b2[e]
                out = out + combine[:, e:e + 1] * y
            return out
        key = jax.random.key(seed)
        ks = jax.random.split(key, 4)
        scale = 1.0 / np.sqrt(D).astype(np.float32)
        return {'input_embeddings': jax.random.normal(ks[0], (B, S, D), jnp.float32), 'router_w': jax.random.normal(ks[1], (NUM_EXPERTS, D), jnp.float32) * scale, 'w1': jax.random.normal(ks[2], (NUM_EXPERTS, D, D), jnp.float32) * scale, 'b1': jnp.zeros((NUM_EXPERTS, D), jnp.float32), 'w2': jax.random.normal(ks[3], (NUM_EXPERTS, D, D), jnp.float32) * scale, 'b2': jnp.zeros((NUM_EXPERTS, D), jnp.float32)}
    _L0_ffn_all = _L0_ffn_setup()
    _L0_ffn_in = {k: v for k, v in _L0_ffn_all.items() if k in ('router_w', 'w1', 'b1', 'w2', 'b2')}
    del _L0_ffn_all
    return {'x': x, 'L0_tok_w': _L0_tok_in['w'], 'L0_tok_b': _L0_tok_in['b'], 'L0_attn_wq': _L0_attn_in['wq'], 'L0_attn_wkv': _L0_attn_in['wkv'], 'L0_attn_wo': _L0_attn_in['wo'], 'L0_attn_q_norm_w': _L0_attn_in['q_norm_w'], 'L0_attn_k_norm_w': _L0_attn_in['k_norm_w'], 'L0_ffn_router_w': _L0_ffn_in['router_w'], 'L0_ffn_w1': _L0_ffn_in['w1'], 'L0_ffn_b1': _L0_ffn_in['b1'], 'L0_ffn_w2': _L0_ffn_in['w2'], 'L0_ffn_b2': _L0_ffn_in['b2']}

def reference(x, L0_tok_w, L0_tok_b, L0_attn_wq, L0_attn_wkv, L0_attn_wo, L0_attn_q_norm_w, L0_attn_k_norm_w, L0_ffn_router_w, L0_ffn_w1, L0_ffn_b1, L0_ffn_w2, L0_ffn_b2):
    import jax
    import jax.numpy as jnp

    def _L0_tok_ref(x, w, b):
        import jax, jax.numpy as jnp
        import numpy as np
        KERNEL_SIZE = 8
        k = KERNEL_SIZE
        B, F, T = x.shape
        pad = -T % k
        if pad:
            x = jnp.pad(x, ((0, 0), (0, 0), (0, pad)))
            T += pad
        nw = T // k
        xp = x.reshape(B, F, nw, k).transpose(0, 2, 3, 1)
        scores = jnp.einsum('bwkf,of->bwko', xp, w) + b
        weights = jax.nn.softmax(scores, axis=2)
        pooled = jnp.sum(xp * weights, axis=2)
        return pooled

    def _L0_attn_ref(x, wq, wkv, wo, q_norm_w, k_norm_w):
        import jax, jax.numpy as jnp
        import numpy as np
        import math
        B, T, D_MODEL = (1, 512, 64)
        N_Q, N_KV = (16, 1)
        D_HEAD = D_MODEL // N_KV
        QPG = N_Q // N_KV
        ROPE_BASE = 10000.0
        WINDOW = 128
        EPS = 1.1920929e-07
        NEG = -1e+30

        def _rope(x, base=ROPE_BASE):
            t, d = (x.shape[-2], x.shape[-1])
            freqs = base ** (-2.0 * jnp.arange(d // 2, dtype=jnp.float32) / d)
            theta = jnp.arange(t, dtype=jnp.float32)[:, None] * freqs[None, :]
            cos, sin = (jnp.cos(theta), jnp.sin(theta))
            x1, x2 = (x[..., 0::2], x[..., 1::2])
            r1 = x1 * cos - x2 * sin
            r2 = x1 * sin + x2 * cos
            return jnp.stack([r1, r2], axis=-1).reshape(x.shape)

        def _rmsnorm(x, w):
            return x * jax.lax.rsqrt(jnp.mean(x * x, axis=-1, keepdims=True) + EPS) * w
        Bx, Tx, C = x.shape
        q = x @ wq.T
        kv = x @ wkv.T
        k, v = (kv[..., :N_KV * D_HEAD], kv[..., N_KV * D_HEAD:])
        q = q.reshape(Bx, Tx, QPG, N_KV, D_HEAD).transpose(0, 2, 3, 1, 4)
        k = k.reshape(Bx, Tx, 1, N_KV, D_HEAD).transpose(0, 2, 3, 1, 4)
        v = v.reshape(Bx, Tx, 1, N_KV, D_HEAD).transpose(0, 2, 3, 1, 4)
        q = _rmsnorm(_rope(q), q_norm_w)
        k = _rmsnorm(_rope(k), k_norm_w)
        rows = jnp.arange(Tx)[:, None]
        cols = jnp.arange(Tx)[None, :]
        mask = (cols <= rows) & (rows - cols <= WINDOW)
        scale = 1.0 / math.sqrt(D_HEAD)
        scores = jnp.einsum('bqgtd,bqgsd->bqgts', q, k) * scale
        scores = jnp.where(mask[None, None, None], scores, NEG)
        attn = jax.nn.softmax(scores, axis=-1)
        out = jnp.einsum('bqgts,bqgsd->bqgtd', attn, v)
        out = out.transpose(0, 3, 1, 2, 4).reshape(Bx, Tx, QPG * N_KV * D_HEAD)
        return out @ wo.T

    def _L0_ffn_ref(input_embeddings, router_w, w1, b1, w2, b2):
        import jax, jax.numpy as jnp
        import numpy as np
        NUM_EXPERTS = 8
        TOP_K = 2
        B, S, D = (8, 2048, 64)

        def _moe(tokens, router_w, w1, b1, w2, b2):
            N = tokens.shape[0]
            E = router_w.shape[0]
            logits = tokens.astype(jnp.float32) @ router_w.astype(jnp.float32).T
            probs = jax.nn.softmax(logits, axis=-1)
            rw, re = jax.lax.top_k(probs, TOP_K)
            if TOP_K > 1:
                rw = rw / jnp.maximum(rw.sum(-1, keepdims=True), 1e-12)
            rw = rw.astype(tokens.dtype)
            combine = jnp.zeros((N, E), tokens.dtype).at[jnp.arange(N)[:, None], re].set(rw)
            out = tokens
            for e in range(E):
                h = jax.nn.gelu(tokens @ w1[e] + b1[e], approximate=False)
                y = h @ w2[e] + b2[e]
                out = out + combine[:, e:e + 1] * y
            return out
        b, s, d = input_embeddings.shape
        tokens = input_embeddings.reshape(b * s, d)
        return _moe(tokens, router_w, w1, b1, w2, b2).reshape(b, s, d)
    h = _L0_tok_ref(x, L0_tok_w, L0_tok_b)
    h = h + _L0_attn_ref(_layernorm(h, axis=-1), L0_attn_wq, L0_attn_wkv, L0_attn_wo, L0_attn_q_norm_w, L0_attn_k_norm_w)
    h = h + _L0_ffn_ref(_layernorm(h, axis=-1), L0_ffn_router_w, L0_ffn_w1, L0_ffn_b1, L0_ffn_w2, L0_ffn_b2)
    return h

_drawn_inputs = setup_inputs


def setup_inputs(seed=0):
    import zlib

    import numpy as np

    out = dict(_drawn_inputs(seed))
    spreads = {'L0_attn_q_norm_w': (1.0, 0.2),
     'L0_attn_k_norm_w': (1.0, 0.2),
     'L0_ffn_b1': (0.0, 0.1),
     'L0_ffn_b2': (0.0, 0.1)}
    factors = {}
    for name, (base, spread) in spreads.items():
        noise = np.random.default_rng([zlib.crc32(name.encode()), seed]).standard_normal(out[name].shape)
        drawn = base * np.exp(spread * noise) if base else spread * noise
        out[name] = jnp.asarray(drawn.astype(out[name].dtype))
    for name, factor in factors.items():
        out[name] = (out[name] * factor).astype(out[name].dtype)
    return out
```

```python
from contextlib import ExitStack

import numpy as np

import concourse.bass as bass
from concourse import mybir

F32 = mybir.dt.float32
F32R = mybir.dt.float32r
I32 = mybir.dt.int32
ALU = mybir.AluOpType
ACT = mybir.ActivationFunctionType
AX = mybir.AxisListType.X

B, F, TIME, K = 64, 64, 256, 8
W = TIME // K
D = F
H = 16
E = 8
P = 128
NPAIR = H // 2
HALVES = 2
RB = B // HALVES
NT = RB * W // P
TOK = NT * P
NJ = B // 2 // HALVES
EPS_LN = 1e-5
EPS_RMS = 1.1920929e-07
NEG = -1e30
RSQRT_MAGIC = 0x5F3759DF
SQ_RING = 4

C_ID, C_COS, C_SIN, C_MASK, C_ROW, C_SELC, C_ONES, C_IDX, C_END = np.cumsum(
    [0, P, D, D, W, 32, (E // 2) * P, NPAIR * 32, E]).tolist()


def shape_constants():
    c = np.zeros((P, C_END), np.float32)
    p = np.arange(P)
    c[:, C_ID:C_COS] = np.eye(P)
    freqs = np.float32(10000.0) ** (np.float32(-2.0) * np.arange(D // 2, dtype=np.float32) / np.float32(D))
    theta = np.arange(W, dtype=np.float32)[:, None] * freqs[None, :].astype(np.float32)
    cos, sin = np.cos(theta).astype(np.float32), np.sin(theta).astype(np.float32)
    c[:, C_COS:C_SIN] = np.repeat(cos, 2, axis=1)[p % W]
    c[:, C_SIN:C_MASK] = (np.repeat(sin, 2, axis=1) * np.tile([-1.0, 1.0], D // 2))[p % W]
    c[:, C_MASK:C_ROW] = np.where(np.arange(W)[None, :] <= (p % W)[:, None], 0.0, NEG)
    q = np.arange(32)
    c[:, C_ROW:C_SELC] = (p[:, None] % 64) == (32 * (q // 16) + q % 16)[None, :]
    for pr in range(E // 2):
        for e2 in range(2):
            rows = [r for r in range(2 * E) if r % E == 2 * pr + e2]
            c[rows, C_SELC + pr * P + 64 * e2:C_SELC + pr * P + 64 * e2 + 64] = 1.0
    for pair in range(NPAIR):
        for h2 in range(2):
            c[64 * h2:64 * h2 + 64, C_ONES + pair * 32 + 2 * pair + h2] = 1.0
    c[:, C_IDX:C_END] = (E - np.arange(E))[None, :]
    rot = np.zeros((P, W, P), np.float32)
    for h2 in range(2):
        for i in range(D // 2):
            a, b = 64 * h2 + 2 * i, 64 * h2 + 2 * i + 1
            rot[a, :, a], rot[b, :, b] = cos[:, i], cos[:, i]
            rot[b, :, a], rot[a, :, b] = -sin[:, i], sin[:, i]
    return c, rot.reshape(P, W * P)


def pe_order():
    jobs = []

    def add(region, *key):
        jobs.append((key, region))

    pair_turn = [0]

    def add01(*key):
        add("P%d" % (pair_turn[0] % 2), *key)
        pair_turn[0] += 1

    def tok(hf, regions):
        add("B5", "score", hf)
        for i in range(4):
            add(regions[i % len(regions)], "wb", hf, i)
        add("B4", "hT", hf)

    tok(0, ["P2", "P0"])
    pair_turn[0] = 1
    add("P2", "xT", 0)
    add("P2", "kv", 0)
    for p in range(NPAIR):
        add01("A", 0, p)
    add("B5", "score", 1)
    for k in range(8):
        add01("D", 0, k)
        if k % 2 == 1:
            add("P2", "wb", 1, k // 2)
        if k == 0:
            add("B5", "ss", 0)
    add("P2", "KT", 0)
    add("B4", "ssT", 0)
    add("B4", "hT", 1)
    attention(jobs, add, add01, 0, {2: [("P2", "xT", 1)], 4: [("P2", "kv", 1)]})
    add("B5", "OP", 0)
    for p in range(NPAIR):
        add01("A", 1, p)
        if p == 1:
            add("B4", "yT", 0)
    add("P2", "KT", 1)
    for k in range(8):
        add01("D", 1, k)
        if k == 0:
            add("B5", "ss", 1)
        if k == 4:
            add("P2", "x2T", 0)
        if k == 5:
            add("B5", "lg", 0)
    add("B4", "ssT", 1)
    attention(jobs, add, add01, 1, {})
    add("P2", "cT", 0)
    for pr in range(4):
        add01("L1", 0, pr)
        add("P2", "cb", 0, pr)
    add("B5", "L2", 0)
    add("B4", "zT", 0)
    add("B5", "OP", 1)
    add("B4", "yT", 1)
    add("P2", "x2T", 1)
    add("B5", "lg", 1)
    for pr in range(2):
        add01("L1", 1, pr)
    add("P2", "cT", 1)
    for pr in range(4):
        if pr >= 2:
            add01("L1", 1, pr)
        add("P2", "cb", 1, pr)
    add("B5", "L2", 1)
    add("B4", "zT", 1)
    return jobs


def attention(jobs, add, add01, hf, extra):
    for T in range(NT + 2):
        if T < NT:
            add01("S", hf, T)
        if T >= 2:
            add("P2", "PV", hf, T - 2)
        if 1 <= T <= NT:
            add("B4", "PT", hf, T - 1)
        for region, *key in extra.get(T, []):
            add(region, *key)


def audio_tower(nc, x, tok_w_t, tok_b, wq_t, wkv_t, wo_t, q_norm_w, k_norm_w, router_t, w1_t, b1_t, w2, b2,
                const, rot, out):
    jobs = pe_order()
    region_of, use_of, uses = {}, {}, {}
    for key, region in jobs:
        uses[region] = uses.get(region, 0) + 1
        region_of[key], use_of[key] = region, uses[region]

    with ExitStack() as ctx:
        def sb(name, shape, dt=F32):
            return ctx.enter_context(nc.sbuf_tensor(name, shape, dt))

        def sem(name):
            return ctx.enter_context(nc.semaphore(name))

        ps = {r: ctx.enter_context(nc.psum_tensor("ps_" + r, [P, 1024], F32)) for r in ("P0", "P1", "P2")}
        ps |= {r: ctx.enter_context(nc.psum_tensor("ps_" + r, [P, 512], F32)) for r in ("B4", "B5")}
        filled = {r: sem("filled_" + r) for r in ps}
        freed = {r: sem("freed_" + r) for r in ps}

        qr_sb = sb("qr_sb", [P, RB, NPAIR, W])
        raw = qr_sb[:, :, :, :].rearrange("p b a t -> p (b a t)")
        wq_raw, wkv_raw, w1_raw, router_raw = (raw[:, a:b] for a, b in ((0, 1024), (1024, 1152), (1152, 1664), (1664, 1672)))
        cst = sb("cst", [P, C_END])
        ident = cst[:, C_ID:C_COS]
        rot_sb = sb("rot_sb", [P, W, P])
        w2_sb = sb("w2_sb", [P, E // 2, D])
        b1_sb = sb("b1_sb", [P, E // 2])
        b2_sb = sb("b2_sb", [P, D])
        norm_w = sb("norm_w", [P, 2, D])
        key_gain = sb("key_gain", [P, D])
        tokb_sb = sb("tokb_sb", [P, 1])
        wz = sb("wz", [P, 64])
        wqT = sb("wqT", [P, 2, H * D], F32R)
        wkvT = sb("wkvT", [P, 2, P], F32R)
        routerT = sb("routerT", [P, 2, E], F32R)
        w1s = sb("w1s", [P, 2, E * D], F32R)
        woT = sb("woT", [P, NPAIR, D])
        row_sel = sb("row_sel", [P, 32, D], F32R)
        expert_sel = sb("expert_sel", [P, E // 2, P], F32R)

        x_sb = sb("x_sb", [P, HALVES * NJ, TIME])
        score_sb = sb("score_sb", [P, TIME])
        pool_w = sb("pool_w", [P, TIME])
        pool_ws = sb("pool_ws", [P, HALVES, TIME], F32R)
        win_stat = sb("win_stat", [P, 3, W])
        prod = sb("prod", [P, 2, 4 * TIME])
        pooledT = sb("pooledT", [P, NJ * W])
        after_x = x_sb[:, :, :].rearrange("p j t -> p (j t)")
        value_block = after_x[:, 0:RB * P].rearrange("p (b m) -> p b m", b=RB)
        prob = after_x[:, 4096:5120].rearrange("p (r g j h s) -> p r g j h s", r=2, g=2, j=4, h=2)
        key_block = after_x[:, 5120:5120 + (RB + 1) * 2 * W].rearrange("p (b s) -> p b s", b=RB + 1)
        y_sb = after_x[:, 7232:7744]
        rq_stat = after_x[:, 7744:8128].rearrange("p (a n) -> p a n", a=3)
        after_prod = prod[:, :, :].rearrange("p r n -> p (r n)")
        probT = after_prod[:, 0:1024].rearrange("p (r q g n) -> p r q g n", r=2, q=2, g=2)
        h2_sb = after_prod[:, 1024:2048].rearrange("p (a n f) -> p a n f", a=HALVES, n=NT)
        gateT = row_sel[:, 0:16, :].rearrange("p a f -> p (a f)")
        h_sb = sb("h_sb", [P, HALVES, NT, D])
        ktmp = sb("ktmp", [P, 3, NT, D])
        dev, sqd = ktmp[:, 0, :, :], ktmp[:, 1, :, :]
        ln_sb = sb("ln_sb", [P, NT, 2, D])
        stat = sb("stat", [P, 8, NT])
        xs = sb("xs", [P, TOK], F32R)
        kv_sb = sb("kv_sb", [P, NT, P])
        kn = sb("kn", [P, NT, 2, D])
        q_sb = sb("q_sb", [P, NPAIR, TOK])
        o_sb = q_sb
        sq_sb = sb("sq_sb", [P, SQ_RING, TOK])
        ssq_sb = sb("ssq_sb", [P, 256])
        rq = sb("rq", [P, HALVES, NT, 2, 4, 2])
        row_stat = sb("row_stat", [P, 2, 3, 16])
        ln2_sb = ln_sb
        xs2 = xs
        rt = sb("rt", [P, 8, NT, E])
        r1 = sb("r1", [P, 6, NT])
        gate = sb("gate", [P, HALVES, NT, 2 * E], F32R)
        hid = raw[:, 0:2048].rearrange("p (r n) -> p r n", r=2)
        hidg = raw[:, 2048:6144].rearrange("p (r n) -> p r n", r=4)
        z_sb = y_sb

        s_cst, s_rot, s_tokw, s_wq, s_wsm, s_wff, s_wo, s_out = (
            sem(n) for n in ("cst_in", "rot_in", "tokw_in", "wq_in", "wsmall_in", "wffn_in", "wo_in", "out_stored"))
        s_x = [[sem(f"x_in{h}{g}") for g in range(2)] for h in range(HALVES)]
        names = ("wz_zero zeroed weights_hi weights_ready selectors dve_link score_shift pool_exp pool_w_ready pooled "
                 "ln_ready xs_hi kn_ready values_in q_squared q_squared_p squares_used logits_ready prob_exp "
                 "prob_sums prob_ready ln2_ready xs2_hi gate_exp gate_ready").split()
        S = {n: sem(n) for n in names}
        block = ctx.enter_context(nc.Block())

        def wait_filled(eng, *key):
            r = region_of[key]
            eng.wait_ge(filled[r], use_of[key])
            return ps[r]

        def is_freed(*key):
            return freed[region_of[key]]

        def wait_freed(eng, *key):
            eng.wait_ge(freed[region_of[key]], use_of[key])

        def square_slot_free(eng, hf, p):
            if p >= SQ_RING:
                eng.wait_ge(S["squares_used"], (NPAIR - 1) * hf + p - SQ_RING + 1)
            elif hf:
                wait_filled(eng, "ss", 0)

        @block.sync
        def _(sp):
            xv = x.rearrange("(j c) f t -> (c f) j t", c=2)
            sp.wait_ge(S["wz_zero"], 1)
            sp.dma_start(wz[0:64, 30:31], tok_w_t).then_inc(s_tokw, 16)
            sp.dma_start(wz[64:128, 31:32], tok_w_t).then_inc(s_tokw, 16)
            sp.dma_start(tokb_sb[:, :], tok_b.rearrange("(a o) -> a o", a=1).to_broadcast([P, 1])).then_inc(s_tokw, 16)
            for hf in range(HALVES):
                for g in range(2):
                    j = NJ * hf + 8 * g
                    sp.dma_start(x_sb[:, j:j + 8, :], xv[:, j:j + 8, :]).then_inc(s_x[hf][g], 16)
            sp.wait_ge(S["zeroed"], 1)
            sp.dma_start(b2_sb[0:E, :], b2).then_inc(s_wff, 16)
            sp.dma_start(b2_sb[E:2 * E, :], b2).then_inc(s_wff, 16)
            ov = out.rearrange("(J j c) w f -> c j w J f", c=2, j=4)
            n = 0
            for hf in range(HALVES):
                wait_freed(sp, "zT", hf)
                r = h2_sb[:, hf, :, :].rearrange("p (J c) f -> p c J f", c=2)
                for c in range(2):
                    for j4 in range(4):
                        sp.dma_start(ov[c, j4, :, 4 * hf:4 * hf + 4, :],
                                     r[32 * j4:32 * j4 + 32, c, :, :]).then_inc(s_out, 16)
                        n += 16
            sp.wait_ge(s_out, n)

        @block.gpsimd
        def _(pool):
            nc.gpsimd.memset(wz[:, :], 0.0).then_inc(S["wz_zero"], 1)
            nc.gpsimd.memset(b2_sb[:, :], 0.0).then_inc(S["zeroed"], 1)
            for hf in range(HALVES):
                for p in range(NPAIR):
                    wait_freed(pool, "A", hf, p)
                    square_slot_free(pool, hf, p)
                    nc.gpsimd.tensor_tensor(sq_sb[:, p % SQ_RING, 0:512], q_sb[:, p, 0:512], q_sb[:, p, 0:512],
                                            ALU.mult).then_inc(S["q_squared_p"], 1)
                if hf == 0:
                    pool.wait_ge(S["pooled"], 8)
                    nc.gpsimd.memset(key_block[:, :, :], 0.0).then_inc(S["zeroed"], 1)
                    nc.gpsimd.memset(value_block[:, :, :], 0.0).then_inc(S["zeroed"], 1)
                    nc.gpsimd.memset(gateT[:, :].bitcast(F32), 0.0).then_inc(S["zeroed"], 1)
                for T in range(NT):
                    n = NT * hf + T
                    pool.wait_ge(S["prob_sums"], n + 1)
                    e = prob[:, n % 2, :, :, :, :].rearrange("p g j h s -> p (g j h) s")
                    nc.gpsimd.tensor_tensor(e, e, row_stat[:, n % 2, 2, :].unsqueeze(2).to_broadcast([P, 16, W]),
                                            ALU.mult).then_inc(S["prob_ready"], 1)

        @block.scalar
        def _(act):
            act.dma_start(cst[:, :], const).then_inc(s_cst, 16)
            for c in range(2):
                r = slice(D * c, D * c + D)
                act.dma_start(wq_raw[r, :], wq_t).then_inc(s_wq, 16)
                act.dma_start(wkv_raw[r, :], wkv_t).then_inc(s_wsm, 16)
                act.dma_start(router_raw[r, :], router_t).then_inc(s_wsm, 16)
            act.dma_start(norm_w[:, 0, :], q_norm_w.rearrange("(a d) -> a d", a=1).to_broadcast([P, D])).then_inc(s_wsm, 16)
            act.dma_start(norm_w[:, 1, :], k_norm_w.rearrange("(a d) -> a d", a=1).to_broadcast([P, D])).then_inc(s_wsm, 16)
            act.dma_start(rot_sb[:, :, :], rot.rearrange("p (t m) -> p t m", t=W)).then_inc(s_rot, 16)
            act.dma_start(w1_raw[0:64, :], w1_t).then_inc(s_wff, 16)
            act.dma_start(w1_raw[64:128, :], w1_t).then_inc(s_wff, 16)
            act.dma_start(w2_sb[:, :, :], w2.rearrange("(a e) f m -> (e f) a m", e=2)).then_inc(s_wff, 16)
            act.dma_start(b1_sb[:, :], b1_t).then_inc(s_wff, 16)
            act.dma_start(woT[:, :, :], wo_t.rearrange("p (a m) -> p a m", a=NPAIR)).then_inc(s_wo, 16)

            def copy(o, i):
                return nc.scalar.activation(o, i, ACT.Copy)

            act.wait_ge(s_wq, 32)
            copy(wqT[:, 0, :], wq_raw).then_inc(S["weights_hi"], 1)

            def pool_exp(hf):
                r = slice(64 * hf, 64 * hf + 64)
                act.wait_ge(S["score_shift"], hf + 1)
                nc.scalar.activation(pool_w[r, :], score_sb[r, :], ACT.Exp).then_inc(S["pool_exp"], 1)

            def h_out(hf):
                t = wait_filled(act, "hT", hf)
                copy(h_sb[:, hf, :, :], t[:, :].rearrange("p (n f) -> p n f", f=D)).then_inc(is_freed("hT", hf), 1)

            def xs_hi(hf):
                t = wait_filled(act, "xT", hf)
                if hf:
                    wait_filled(act, "A", 0, NPAIR - 1)
                copy(xs[:, :], t[:, :]).then_inc(S["xs_hi"], 1)

            def kv_out(hf):
                t = wait_filled(act, "kv", hf)
                if hf:
                    act.wait_ge(S["values_in"], 1)
                copy(kv_sb[:, :, :], t[:, :].rearrange("p (n f) -> p n f", f=P)).then_inc(is_freed("kv", hf), 1)

            def keys_in(hf):
                t = wait_filled(act, "KT", hf)
                act.wait_ge(S["zeroed"], 2)
                if hf:
                    wait_filled(act, "S", 0, NT - 1)
                for h2 in range(2):
                    r = slice(64 * h2, 64 * h2 + 64)
                    i = copy(key_block[r, 0:RB, W * h2:W * h2 + W], t[r, :].rearrange("p (b s) -> p b s", s=W))
                i.then_inc(is_freed("KT", hf), 1)

            def q_out(hf, p):
                t = wait_filled(act, "A", hf, p)
                if hf and p == 0:
                    wait_filled(act, "OP", 0)
                copy(q_sb[:, p, :], t[:, :]).then_inc(is_freed("A", hf, p), 1)

            def q_square(hf, p):
                wait_freed(act, "A", hf, p)
                square_slot_free(act, hf, p)
                nc.scalar.activation(sq_sb[:, p % SQ_RING, 512:1024], q_sb[:, p, 512:1024],
                                     ACT.Square).then_inc(S["q_squared"], 1)

            def attn(hf, extra):
                for T in range(NT + 2):
                    if 1 <= T <= NT:
                        n = NT * hf + T - 1
                        act.wait_ge(S["logits_ready"], n + 1)
                        e = prob[:, n % 2, :, :, :, :].rearrange("p g j h s -> p (g j h s)")
                        nc.scalar.activation(e, e, ACT.Exp).then_inc(S["prob_exp"], 1)
                    if T >= 2:
                        t = wait_filled(act, "PV", hf, T - 2)
                        if T == 2 and hf:
                            wait_filled(act, "D", 1, 7)
                        elif T == 2:
                            wait_filled(act, "D", 0, 7)
                        o = o_sb[:, :, P * (T - 2):P * (T - 1)].rearrange("p a (j t) -> p j a t", j=4)
                        copy(o, t[:, :].rearrange("p (j a t) -> p j a t", j=4, a=NPAIR))\
                            .then_inc(is_freed("PV", hf, T - 2), 1)
                    if 1 <= T <= NT:
                        n = NT * hf + T - 1
                        t = wait_filled(act, "PT", hf, T - 1)
                        copy(probT[:, n % 2, :, :, :], t[:, :].rearrange("p (g r n) -> p r g n", g=2, r=2))\
                            .then_inc(is_freed("PT", hf, T - 1), 1)
                    for f in extra.get(T, []):
                        f()

            def y_out(hf):
                t = wait_filled(act, "OP", hf)
                if hf:
                    wait_filled(act, "zT", 0)
                copy(y_sb[:, :], t[:, :]).then_inc(is_freed("OP", hf), 1)

            def xs2_hi(hf):
                t = wait_filled(act, "x2T", hf)
                wait_filled(act, *(("L1", 0, 3) if hf else ("A", 1, NPAIR - 1)))
                copy(xs2[:, :], t[:, :]).then_inc(S["xs2_hi"], 1)

            def gate_exp(hf):
                wait_freed(act, "lg", hf)
                nc.scalar.activation(rt[:, 0, :, :], rt[:, 0, :, :], ACT.Exp).then_inc(S["gate_exp"], 1)

            def gateT_out(hf):
                t = wait_filled(act, "cT", hf)
                if hf:
                    wait_filled(act, "L2", 0)
                act.wait_ge(S["zeroed"], 4)
                copy(gateT[0:2 * E, :], t[0:2 * E, :]).then_inc(is_freed("cT", hf), 1)

            def gelu(hf, pr):
                n = 4 * hf + pr
                t = wait_filled(act, "L1", hf, pr)
                if n == 0:
                    act.wait_ge(s_wff, 96)
                if n >= 2:
                    wait_freed(act, "cb", (n - 2) // 4, (n - 2) % 4)
                nc.scalar.activation(hid[:, n % 2, :], t[:, :], ACT.Gelu, bias=b1_sb[:, pr:pr + 1])\
                    .then_inc(is_freed("L1", hf, pr), 1)

            def z_out(hf):
                t = wait_filled(act, "L2", hf)
                wait_filled(act, "yT", hf)
                copy(z_sb[:, :], t[:, :]).then_inc(is_freed("L2", hf), 1)

            pool_exp(0)
            h_out(0)
            xs_hi(0)
            kv_out(0)
            for p in range(NPAIR):
                q_out(0, p)
            for p in range(NPAIR):
                q_square(0, p)
                if p == 2:
                    pool_exp(1)
            keys_in(0)
            h_out(1)
            attn(0, {2: [lambda: xs_hi(1)], 4: [lambda: kv_out(1)]})
            y_out(0)
            for p in range(NPAIR):
                q_out(1, p)
            keys_in(1)
            for p in range(NPAIR):
                q_square(1, p)
            xs2_hi(0)
            gate_exp(0)
            attn(1, {})
            gateT_out(0)
            for pr in range(4):
                gelu(0, pr)
            z_out(0)
            y_out(1)
            xs2_hi(1)
            gate_exp(1)
            gelu(1, 0)
            gelu(1, 1)
            gateT_out(1)
            gelu(1, 2)
            gelu(1, 3)
            z_out(1)

        @block.vector
        def _(dve):
            chain = [0]

            def link(ins):
                chain[0] += 1
                ins.then_inc(S["dve_link"], 1)
                dve.wait_ge(S["dve_link"], chain[0])

            tt, ts, red, stt = (nc.vector.tensor_tensor, nc.vector.tensor_scalar, nc.vector.tensor_reduce,
                                nc.vector.scalar_tensor_tensor)

            def bc(a, n):
                return a.unsqueeze(len(a.shape)).to_broadcast([*a.shape, n])

            def rsqrt(y, v, t):
                link(ts(t.bitcast(I32), v.bitcast(I32), 1, None, ALU.logical_shift_right))
                link(ts(y.bitcast(I32), t.bitcast(I32), -1.0, float(RSQRT_MAGIC), ALU.mult, ALU.add))
                for _ in range(3):
                    link(tt(t, y, y, ALU.mult))
                    link(stt(out=t, in0=t, scalar=-0.5, in1=v, op0=ALU.mult, op1=ALU.mult))
                    link(stt(out=y, in0=t, scalar=1.5, in1=y, op0=ALU.add, op1=ALU.mult))

            dve.wait_ge(s_cst, 16)
            nc.vector.tensor_copy(row_sel[:, :, :], bc(cst[:, C_ROW:C_SELC], D)).then_inc(S["selectors"], 1)
            nc.vector.tensor_copy(expert_sel[:, :, :], cst[:, C_SELC:C_ONES].rearrange("p (a n) -> p a n", n=P))\
                .then_inc(S["selectors"], 1)

            def split(parts, raw_w):
                link(nc.vector.tensor_copy(parts[:, 0, :], raw_w))
                return tt(parts[:, 1, :], raw_w, parts[:, 0, :].bitcast(F32), ALU.subtract)

            def attention_weights():
                dve.wait_ge(s_wsm, 16 * 6)
                split(wkvT, wkv_raw).then_inc(S["weights_ready"], 1)
                split(routerT, router_raw).then_inc(S["weights_ready"], 1)
                stt(out=key_gain[:, :], in0=norm_w[:, 0, :], scalar=float(D) ** -0.5, in1=norm_w[:, 1, :],
                    op0=ALU.mult, op1=ALU.mult).then_inc(S["weights_ready"], 1)
                dve.wait_ge(S["weights_hi"], 1)
                tt(wqT[:, 1, :], wq_raw, wqT[:, 0, :].bitcast(F32), ALU.subtract).then_inc(S["weights_ready"], 1)

            def w1_split():
                dve.wait_ge(s_wff, 96)
                split(w1s, w1_raw).then_inc(S["weights_ready"], 1)

            def pool_softmax(hf):
                r = slice(64 * hf, 64 * hf + 64)
                t = wait_filled(dve, "score", hf)
                sc, pw = score_sb[r, :], pool_w[r, :]
                mx, sm, inv = (win_stat[r, i, :] for i in range(3))
                dve.wait_ge(s_tokw, 48)
                ts(sc, t[r, 0:TIME], tokb_sb[r, :], None, ALU.add).then_inc(is_freed("score", hf), 1)
                wait_freed(dve, "score", hf)
                v = sc.rearrange("p (w k) -> p w k", k=K)
                link(red(mx, v, AX, ALU.max))
                tt(v, v, bc(mx, K), ALU.subtract).then_inc(S["score_shift"], 1)
                dve.wait_ge(S["pool_exp"], hf + 1)
                v = pw.rearrange("p (w k) -> p w k", k=K)
                link(red(sm, v, AX, ALU.add))
                link(nc.vector.reciprocal(inv, sm))
                link(tt(v, v, bc(inv, K), ALU.mult))
                other = slice(64 - 64 * hf, 128 - 64 * hf)
                link(nc.vector.tensor_copy(pool_ws[r, hf, :], pw))
                tt(pool_ws[other, hf, :], pw, pool_ws[r, hf, :].bitcast(F32), ALU.subtract)\
                    .then_inc(S["pool_w_ready"], 1)

            def pool_sum(hf, i):
                n = 4 * hf + i
                t = wait_filled(dve, "wb", hf, i)
                j = NJ * hf + 4 * i
                pr = prod[:, n % 2, :]
                tt(pr, t[:, :], x_sb[:, j:j + 4, :].rearrange("p j t -> p (j t)"), ALU.mult)\
                    .then_inc(is_freed("wb", hf, i), 1)
                wait_freed(dve, "wb", hf, i)
                if hf and i == 0:
                    wait_filled(dve, "hT", 0)
                i_ = red(pooledT[:, 4 * W * i:4 * W * (i + 1)], pr.rearrange("p (w k) -> p w k", k=K), AX, ALU.add)
                i_.then_inc(S["pooled"], 1)

            def layernorm(o, h):
                sm, nm, ss, v, y, t = (stat[:, i, 0:NT] for i in range(6))
                link(red(sm, h, AX, ALU.add))
                link(ts(nm, sm, 1.0 / D, None, ALU.mult))
                link(tt(dev, h, bc(nm, D), ALU.subtract))
                link(tt(sqd, dev, dev, ALU.mult))
                link(red(ss, sqd, AX, ALU.add))
                link(ts(v, ss, 1.0 / D, EPS_LN, ALU.mult, ALU.add))
                rsqrt(y, v, t)
                d2 = dev.unsqueeze(2).to_broadcast([P, NT, 2, D])
                y2 = y.unsqueeze(2).unsqueeze(3).to_broadcast([P, NT, 2, D])
                return tt(o, d2, y2, ALU.mult)

            def ln1(hf):
                wait_freed(dve, "hT", hf)
                if hf:
                    wait_filled(dve, "xT", 0)
                layernorm(ln_sb[:, :, :, :], h_sb[:, hf, :, :]).then_inc(S["ln_ready"], 1)

            def xs_lo(hf):
                t = wait_filled(dve, "xT", hf)
                dve.wait_ge(S["xs_hi"], hf + 1)
                tt(xs[64:128, :], t[64:128, :], xs[64:128, :].bitcast(F32), ALU.subtract)\
                    .then_inc(is_freed("xT", hf), 1)

            def keys(hf):
                if hf == 0:
                    dve.wait_ge(S["weights_ready"], 3)
                wait_freed(dve, "kv", hf)
                k = kv_sb[:, :, 0:D]
                a, b, c = (ktmp[:, i, :, :] for i in range(3))
                tab = lambda o: cst[:, o:o + D].unsqueeze(1).to_broadcast([P, NT, D])
                link(tt(a, k, tab(C_COS), ALU.mult))
                bv = b.rearrange("p n (i c) -> p n i c", c=2)
                kvw = kv_sb[:, :, 0:D].rearrange("p n (i c) -> p n i c", c=2)
                sv = tab(C_SIN).rearrange("p n (i c) -> p n i c", c=2)
                for cc in range(2):
                    link(tt(bv[:, :, :, cc], kvw[:, :, :, 1 - cc], sv[:, :, :, cc], ALU.mult))
                link(tt(a, a, b, ALU.add))
                link(tt(c, a, a, ALU.mult))
                ss, v, y, t = (stat[:, i, 0:NT] for i in range(4))
                link(red(ss, c, AX, ALU.add))
                link(ts(v, ss, 1.0 / D, EPS_RMS, ALU.mult, ALU.add))
                rsqrt(y, v, t)
                link(tt(a, a, bc(y, D), ALU.mult))
                if hf:
                    wait_filled(dve, "KT", 0)
                g = key_gain[:, :].unsqueeze(1).unsqueeze(1).to_broadcast([P, NT, 2, D])
                tt(kn[:, :, :, :], a.unsqueeze(2).to_broadcast([P, NT, 2, D]), g, ALU.mult)\
                    .then_inc(S["kn_ready"], 1)

            def values_in(hf):
                dve.wait_ge(S["zeroed"], 3)
                if hf:
                    wait_filled(dve, "PV", 0, NT - 1)
                vb = value_block[:, :, :].rearrange("p (n j) m -> p n j m", j=4)
                for j4 in range(4):
                    for h2 in range(2):
                        q = 2 * (j4 % 2) + h2
                        i = nc.vector.tensor_copy(vb[32 * q:32 * q + 32, :, j4, D * h2:D * h2 + D],
                                                  kv_sb[32 * j4:32 * j4 + 32, :, D:2 * D])
                i.then_inc(S["values_in"], 1)

            def qr_out(hf, k):
                t = wait_filled(dve, "D", hf, k)
                if hf and k == 0:
                    wait_filled(dve, "S", 0, NT - 1)
                o = qr_sb[:, :, :, 4 * k:4 * k + 4].rearrange("p b a t -> p t a b")
                nc.vector.tensor_copy(o, t[:, :].rearrange("p (t a b) -> p t a b", t=4, a=NPAIR))\
                    .then_inc(is_freed("D", hf, k), 1)

            def ssq_out(hf):
                t = wait_filled(dve, "ss", hf)
                nc.vector.tensor_copy(ssq_sb[:, :], t[:, 0:256]).then_inc(is_freed("ss", hf), 1)

            def query_scales(hf):
                t = wait_filled(dve, "ssT", hf)
                v, y, tmp = (rq_stat[:, i, :] for i in range(3))
                tv = t[:, 0:256].rearrange("p (i c h) -> p c i h", i=2, c=4)[:, :, :, 0:H]
                link(ts(v.rearrange("p (c i h) -> p c i h", c=4, i=2), tv, 1.0 / D, EPS_RMS, ALU.mult, ALU.add))
                rsqrt(y, v, tmp)
                yv = y.rearrange("p (n g a h) -> p n g a h", n=NT, g=2, a=4)
                for j4 in range(4):
                    for a in range(4):
                        i = nc.vector.tensor_copy(rq[32 * a:32 * a + 32, hf, :, :, j4, :],
                                                  yv[32 * j4:32 * j4 + 32, :, :, a, :])
                i.then_inc(is_freed("ssT", hf), 1)
                wait_freed(dve, "ssT", hf)

            def logits(hf, T):
                n = NT * hf + T
                t = wait_filled(dve, "S", hf, T)
                if n >= 2:
                    dve.wait_ge(filled["B4"], use_of["PT", (n - 2) // NT, (n - 2) % NT])
                e8 = prob[:, n % 2, :, :, :, :].rearrange("p g j h s -> p (g j) h s")
                e16 = prob[:, n % 2, :, :, :, :].rearrange("p g j h s -> p (g j h) s")
                sv = t[:, :].rearrange("p (n x) -> p n x", x=P)[:, :, 0:2 * W].rearrange("p n (h s) -> p n h s", h=2)
                m = cst[:, C_MASK:C_ROW].unsqueeze(1).unsqueeze(1).to_broadcast([P, 8, 2, W])
                tt(e8, sv, m, ALU.add).then_inc(is_freed("S", hf, T), 1)
                wait_freed(dve, "S", hf, T)
                mx = row_stat[:, n % 2, 0, :]
                link(red(mx, e16, AX, ALU.max))
                link(tt(e16, e16, bc(mx, W), ALU.subtract))
                r = rq[:, hf, T, :, :, :].rearrange("p g j h -> p (g j h)")
                tt(e16, e16, bc(r, W), ALU.mult).then_inc(S["logits_ready"], 1)

            def sums(hf, T):
                n = NT * hf + T
                dve.wait_ge(S["prob_exp"], n + 1)
                e16 = prob[:, n % 2, :, :, :, :].rearrange("p g j h s -> p (g j h) s")
                link(red(row_stat[:, n % 2, 1, :], e16, AX, ALU.add))
                nc.vector.reciprocal(row_stat[:, n % 2, 2, :], row_stat[:, n % 2, 1, :]).then_inc(S["prob_sums"], 1)

            def attn(hf, extra):
                for T in range(NT + 1):
                    if T >= 1:
                        sums(hf, T - 1)
                    if T < NT:
                        logits(hf, T)
                    for f in extra.get(T, []):
                        f()

            def ln2(hf):
                t = wait_filled(dve, "yT", hf)
                tv = t[:, :].rearrange("p (i c m) -> p c i m", i=4, c=2)
                h2 = h2_sb[:, hf, :, :]
                tt(h2.rearrange("p (c i) m -> p c i m", c=2), tv,
                   h_sb[:, hf, :, :].rearrange("p (c i) m -> p c i m", c=2), ALU.add).then_inc(is_freed("yT", hf), 1)
                wait_freed(dve, "yT", hf)
                wait_filled(dve, *(("x2T", 0) if hf else ("xT", 1)))
                layernorm(ln2_sb[:, :, :, :], h2).then_inc(S["ln2_ready"], 1)
                dve.wait_ge(S["ln2_ready"], hf + 1)
                link(tt(h2, h2, ln2_sb[:, :, 0, :], ALU.add))

            def xs2_lo(hf):
                t = wait_filled(dve, "x2T", hf)
                dve.wait_ge(S["xs2_hi"], hf + 1)
                tt(xs2[64:128, :], t[64:128, :], xs2[64:128, :].bitcast(F32), ALU.subtract)\
                    .then_inc(is_freed("x2T", hf), 1)

            def router(hf):
                t = wait_filled(dve, "lg", hf)
                lg = t[:, 0:NT * E].rearrange("p (n e) -> p n e", e=E)
                p_, e1, s1, o1, p2, e2, o2, cc = (rt[:, i, :, :] for i in range(8))
                m0, sm, m1, m2, x1, dn = (r1[:, i, :] for i in range(6))
                idx = cst[:, C_IDX:C_END].unsqueeze(1).to_broadcast([P, NT, E])
                link(red(m0, lg, AX, ALU.max))
                tt(p_, lg, bc(m0, E), ALU.subtract).then_inc(is_freed("lg", hf), 1)
                return p_, e1, s1, o1, p2, e2, o2, cc, m0, sm, m1, m2, x1, dn, idx

            def top2(hf, v):
                p_, e1, s1, o1, p2, e2, o2, cc, m0, sm, m1, m2, x1, dn, idx = v
                dve.wait_ge(S["gate_exp"], hf + 1)
                link(red(sm, p_, AX, ALU.add))
                link(nc.vector.reciprocal(dn, sm))
                link(tt(p_, p_, bc(dn, E), ALU.mult))

                def largest(q, m, eq, o):
                    link(red(m, q, AX, ALU.max))
                    link(tt(eq, q, bc(m, E), ALU.is_equal))
                    link(tt(eq, eq, idx, ALU.mult))
                    link(red(x1, eq, AX, ALU.max))
                    link(tt(o, eq, bc(x1, E), ALU.is_equal))

                largest(p_, m1, e1, o1)
                link(stt(out=p2, in0=o1, scalar=-4.0, in1=p_, op0=ALU.mult, op1=ALU.add))
                largest(p2, m2, e2, o2)
                link(tt(cc, o1, o2, ALU.add))
                link(tt(cc, cc, p_, ALU.mult))
                link(tt(sm, m1, m2, ALU.add))
                link(ts(sm, sm, 1e-12, None, ALU.max))
                link(nc.vector.reciprocal(dn, sm))
                link(tt(cc, cc, bc(dn, E), ALU.mult))
                link(nc.vector.tensor_copy(gate[:, hf, :, 0:E], cc))
                tt(gate[:, hf, :, E:2 * E], cc, gate[:, hf, :, 0:E].bitcast(F32), ALU.subtract)\
                    .then_inc(S["gate_ready"], 1)

            def gate_hidden(hf, pr):
                n = 4 * hf + pr
                t = wait_filled(dve, "cb", hf, pr)
                wait_freed(dve, "L1", hf, pr)
                if hf and pr == 0:
                    wait_filled(dve, "L2", 0)
                tt(hidg[:, pr, :], t[:, :], hid[:, n % 2, :], ALU.mult).then_inc(is_freed("cb", hf, pr), 1)

            def finish(hf):
                t = wait_filled(dve, "zT", hf)
                tv = t[:, :].rearrange("p (i c m) -> p c i m", i=4, c=2)
                r = h2_sb[:, hf, :, :].rearrange("p (c i) m -> p c i m", c=2)
                tt(r, tv, r, ALU.add).then_inc(is_freed("zT", hf), 1)

            def blocks():
                attention_weights()
                pool_softmax(0)
                for i in range(4):
                    pool_sum(0, i)
                ln1(0)
                xs_lo(0)
                keys(0)
                w1_split()
                pool_softmax(1)
                for k in range(8):
                    qr_out(0, k)
                    if k % 2 == 1:
                        pool_sum(1, k // 2)
                    if k == 5:
                        ssq_out(0)
                query_scales(0)
                values_in(0)
                attn(0, {0: [lambda: ln1(1)], 2: [lambda: xs_lo(1)], 5: [lambda: keys(1)]})
                values_in(1)
                ln2(0)
                r = []
                for k in range(8):
                    qr_out(1, k)
                    if k == 4:
                        ssq_out(1)
                        xs2_lo(0)
                    if k == 5:
                        r.append(router(0))
                query_scales(1)
                attn(1, {2: [lambda: top2(0, r[0])]})
                for pr in range(4):
                    gate_hidden(0, pr)
                finish(0)
                ln2(1)
                xs2_lo(1)
                top2(1, router(1))
                for pr in range(4):
                    gate_hidden(1, pr)
                finish(1)

            blocks()

        @block.tensor
        def _(pe):
            mm, turn = nc.tensor.matmul, nc.tensor.transpose

            def claim(*key):
                r = region_of[key]
                if use_of[key] > 1:
                    pe.wait_ge(freed[r], use_of[key] - 1)
                return ps[r]

            def done(ins, *key):
                ins.then_inc(filled[region_of[key]], 1)

            def score(hf):
                pe.wait_ge(s_tokw, 48)
                o = claim("score", hf)
                for g in range(2):
                    pe.wait_ge(s_x[hf][g], 16)
                    for jj in range(8):
                        i = mm(o[64 * hf + 32 * g:64 * hf + 32 * g + 32, 0:TIME], wz[:, 30 - 2 * jj:62 - 2 * jj],
                               x_sb[:, NJ * hf + 8 * g + jj, :], start=jj == 0, stop=jj == 7)
                done(i, "score", hf)

            def wb(hf, q):
                pe.wait_ge(S["selectors"], 1)
                pe.wait_ge(S["pool_w_ready"], hf + 1)
                o = claim("wb", hf, q)
                for j in range(4):
                    jj = 4 * q + j
                    i = mm(o[:, TIME * j:TIME * (j + 1)], row_sel[:, 2 * jj:2 * jj + 2, :].rearrange("p a f -> p (a f)"),
                           pool_ws[:, hf, :], start=True, stop=True)
                done(i, "wb", hf, q)

            def hT(hf):
                pe.wait_ge(S["pooled"], 4 * (hf + 1))
                o = claim("hT", hf)
                for j in range(4):
                    i = turn(o[:, P * j:P * j + P], pooledT[:, P * j:P * j + P], ident)
                done(i, "hT", hf)

            def xT(hf):
                pe.wait_ge(S["ln_ready"], hf + 1)
                o = claim("xT", hf)
                for T in range(NT):
                    i = turn(o[:, P * T:P * T + P], ln_sb[:, T, :, :].rearrange("p c d -> p (c d)"), ident)
                done(i, "xT", hf)

            def kv(hf):
                wait_freed(pe, "xT", hf)
                pe.wait_ge(S["weights_ready"], 1)
                o = claim("kv", hf)
                for T in range(NT):
                    for part in range(2):
                        i = mm(o[:, P * T:P * T + P], xs[:, P * T:P * T + P], wkvT[:, part, :],
                               start=part == 0, stop=part == 1)
                done(i, "kv", hf)

            def A(hf, p):
                pe.wait_ge(S["weights_ready"], 4)
                wait_freed(pe, "xT", hf)
                o = claim("A", hf, p)
                for part in range(2):
                    for c in range(2):
                        i = mm(o[:, 512 * c:512 * c + 512], wqT[:, part, P * p:P * p + P], xs[:, 512 * c:512 * c + 512],
                               start=part == 0, stop=part == 1)
                done(i, "A", hf, p)

            def KT(hf):
                pe.wait_ge(S["kn_ready"], hf + 1)
                o = claim("KT", hf)
                for T in range(NT):
                    i = turn(o[:, P * T:P * T + P], kn[:, T, :, :].rearrange("p c d -> p (c d)"), ident)
                done(i, "KT", hf)

            def square_sums(hf, p):
                pe.wait_ge(S["q_squared_p"], NPAIR * hf + p + 1)
                pe.wait_ge(S["q_squared"], NPAIR * hf + p + 1)
                o = claim("ss", hf) if p == 0 else ps[region_of["ss", hf]]
                for c in range(4):
                    i = mm(o[32 * c:32 * c + 32, 0:256], cst[:, C_ONES + 32 * p:C_ONES + 32 * p + 32],
                           sq_sb[:, p % SQ_RING, 256 * c:256 * c + 256], start=p == 0, stop=p == NPAIR - 1)
                if p < NPAIR - 1:
                    i.then_inc(S["squares_used"], 1)
                else:
                    done(i, "ss", hf)

            def ssT(hf):
                wait_freed(pe, "ss", hf)
                o = claim("ssT", hf)
                for j in range(2):
                    i = turn(o[:, P * j:P * j + P], ssq_sb[:, P * j:P * j + P], ident)
                done(i, "ssT", hf)

            def Dj(hf, k):
                pe.wait_ge(s_rot, 16)
                if k == 0:
                    wait_freed(pe, "A", hf, NPAIR - 2)
                    wait_freed(pe, "A", hf, NPAIR - 1)
                o = claim("D", hf, k)
                qv = q_sb[:, :, :].rearrange("p a (b t) -> p a b t", t=W)
                for t in range(4):
                    i = mm(o[:, 256 * t:256 * t + 256], rot_sb[:, 4 * k + t, :], qv[:, :, :, 4 * k + t],
                           start=True, stop=True)
                done(i, "D", hf, k)
                for p in {1: (0, 1), 2: (2, 3), 3: (4, 5), 4: (6, 7)}.get(k, ()):
                    square_sums(hf, p)

            def Sj(hf, T):
                if T == 0:
                    wait_freed(pe, "D", hf, 7)
                    wait_freed(pe, "KT", hf)
                o = claim("S", hf, T)
                for g in range(2):
                    for j4 in range(4):
                        b = 4 * T + j4
                        i = mm(o[:, 512 * g + P * j4:512 * g + P * j4 + P],
                               qr_sb[:, b, 4 * g:4 * g + 4, :].rearrange("p a t -> p (a t)"),
                               key_block[:, b:b + 2, :].rearrange("p b s -> p (b s)"), start=True, stop=True)
                done(i, "S", hf, T)

            def PT(hf, T):
                n = NT * hf + T
                pe.wait_ge(S["prob_ready"], n + 1)
                o = claim("PT", hf, T)
                for g in range(2):
                    for r in range(2):
                        c = P * (2 * g + r)
                        i = turn(o[:, c:c + P], prob[:, n % 2, g, 2 * r:2 * r + 2, :, :].rearrange("p j h s -> p (j h s)"),
                                 ident)
                done(i, "PT", hf, T)

            def PV(hf, T):
                n = NT * hf + T
                wait_freed(pe, "PT", hf, T)
                pe.wait_ge(S["values_in"], hf + 1)
                o = claim("PV", hf, T)
                for j4 in range(4):
                    i = mm(o[:, 256 * j4:256 * j4 + 256], value_block[:, 4 * T + j4, :],
                           probT[:, n % 2, j4 // 2, :, :].rearrange("p g n -> p (g n)"), start=True, stop=True)
                done(i, "PV", hf, T)

            def OP(hf):
                wait_freed(pe, "PV", hf, NT - 1)
                pe.wait_ge(s_wo, 16)
                o = claim("OP", hf)
                for a in range(NPAIR):
                    for c in range(2):
                        i = mm(o[64 * c:64 * c + 64, :], woT[:, a, :], o_sb[:, a, 512 * c:512 * c + 512],
                               start=a == 0, stop=a == NPAIR - 1)
                done(i, "OP", hf)

            def turned(src, src_key, *key):
                wait_freed(pe, *src_key)
                o = claim(*key)
                for j in range(4):
                    i = turn(o[:, P * j:P * j + P], src[:, P * j:P * j + P], ident)
                done(i, *key)

            def x2T(hf):
                pe.wait_ge(S["ln2_ready"], hf + 1)
                o = claim("x2T", hf)
                for T in range(NT):
                    i = turn(o[:, P * T:P * T + P], ln2_sb[:, T, :, :].rearrange("p c d -> p (c d)"), ident)
                done(i, "x2T", hf)

            def lg(hf):
                wait_freed(pe, "x2T", hf)
                o = claim("lg", hf)
                for T in range(NT):
                    for part in range(2):
                        i = mm(o[:, E * T:E * T + E], xs2[:, P * T:P * T + P], routerT[:, part, :],
                               start=part == 0, stop=part == 1)
                done(i, "lg", hf)

            def cT(hf):
                pe.wait_ge(S["gate_ready"], hf + 1)
                o = claim("cT", hf)
                for T in range(NT):
                    i = turn(o[0:2 * E, P * T:P * T + P], gate[:, hf, T, :].bitcast(F32), ident)
                done(i, "cT", hf)

            def L1(hf, pr):
                wait_freed(pe, "x2T", hf)
                pe.wait_ge(S["weights_ready"], 5)
                o = claim("L1", hf, pr)
                for part in range(2):
                    for c in range(2):
                        i = mm(o[:, 512 * c:512 * c + 512], w1s[:, part, P * pr:P * pr + P],
                               xs2[:, 512 * c:512 * c + 512], start=part == 0, stop=part == 1)
                done(i, "L1", hf, pr)

            def cb(hf, pr):
                pe.wait_ge(S["selectors"], 2)
                wait_freed(pe, "cT", hf)
                o = claim("cb", hf, pr)
                for c in range(2):
                    i = mm(o[:, 512 * c:512 * c + 512], expert_sel[:, pr, :], gateT[:, 512 * c:512 * c + 512],
                           start=True, stop=True)
                done(i, "cb", hf, pr)

            def L2(hf):
                pe.wait_ge(s_wff, 96)
                o = claim("L2", hf)
                for c in range(2):
                    mm(o[64 * c:64 * c + 64, :], b2_sb[:, :], gateT[:, 512 * c:512 * c + 512].bitcast(F32),
                       start=True, stop=False)
                for pr in range(4):
                    wait_freed(pe, "cb", hf, pr)
                    for c in range(2):
                        i = mm(o[64 * c:64 * c + 64, :], w2_sb[:, pr, :], hidg[:, pr, 512 * c:512 * c + 512],
                               start=False, stop=pr == 3)
                done(i, "L2", hf)

            run = {"score": score, "wb": wb, "hT": hT, "xT": xT, "kv": kv, "A": A,
                   "KT": KT, "ss": lambda hf: None, "ssT": ssT, "D": Dj, "S": Sj, "PT": PT, "PV": PV, "OP": OP,
                   "yT": lambda hf: turned(y_sb, ("OP", hf), "yT", hf), "x2T": x2T, "lg": lg, "cT": cT, "L1": L1,
                   "cb": cb, "L2": L2, "zT": lambda hf: turned(z_sb, ("L2", hf), "zT", hf)}
            for key, _ in jobs:
                run[key[0]](*key[1:])


def kernel(**inputs):
    import concourse.bacc as bacc
    from concourse.bass_utils import run_bass_kernel_spmd

    nc = bacc.Bacc("TRN2", target_bir_lowering=False, num_devices=1)
    a = {name.removeprefix("L0_"): np.asarray(v) for name, v in inputs.items()}
    const, rot = shape_constants()
    arrays = {
        "x": a["x"], "tok_w_t": a["tok_w"].T, "tok_b": a["tok_b"], "wq_t": a["attn_wq"].T, "wkv_t": a["attn_wkv"].T,
        "wo_t": a["attn_wo"].reshape(D, NPAIR, P).transpose(2, 1, 0).reshape(P, NPAIR * D),
        "q_norm_w": a["attn_q_norm_w"], "k_norm_w": a["attn_k_norm_w"], "router_t": a["ffn_router_w"].T,
        "w1_t": a["ffn_w1"].transpose(1, 0, 2).reshape(D, E * D),
        "b1_t": a["ffn_b1"].reshape(E // 2, P).T, "w2": a["ffn_w2"], "b2": a["ffn_b2"], "const": const, "rot": rot}
    arrays = {name: np.ascontiguousarray(v) for name, v in arrays.items()}
    args = [nc.dram_tensor(name, v.shape, mybir.dt.from_np(v.dtype), kind="ExternalInput").ap()
            for name, v in arrays.items()]
    args.append(nc.dram_tensor("out", (B, W, F), F32, kind="ExternalOutput").ap())
    audio_tower(nc, *args)
    return run_bass_kernel_spmd(nc, [arrays], core_ids=[0]).results[0]["out"]
```

```python
from contextlib import ExitStack

import numpy as np

import concourse.bass as bass
from concourse import mybir

F32 = mybir.dt.float32
F32R = mybir.dt.float32r
I32 = mybir.dt.int32
ALU = mybir.AluOpType
ACT = mybir.ActivationFunctionType
AX = mybir.AxisListType.X

B, F, TIME, K = 64, 64, 256, 8
W = TIME // K
D = F
H = 16
E = 8
P = 128
NPAIR = H // 2
HALVES = 2
RB = B // HALVES
NT = RB * W // P
TOK = NT * P
NJ = B // 2 // HALVES
EPS_LN = 1e-5
EPS_RMS = 1.1920929e-07
NEG = -1e30
RSQRT_MAGIC = 0x5F3759DF
SEG = [(0, NT), (NT, NT // 2), (NT + NT // 2, NT // 2)]
GPSIMD_SUMS = [(2,), (1, 2)]
SQ_RING = 4
PROB_RING = 4

C_ID, C_COS, C_SIN, C_MASK, C_ROW, C_SELC, C_ONES, C_IDX, C_END = np.cumsum(
    [0, P, D, D, W, 32, (E // 2) * P, NPAIR * 32, E]).tolist()


def shape_constants():
    c = np.zeros((P, C_END), np.float32)
    p = np.arange(P)
    c[:, C_ID:C_COS] = np.eye(P)
    freqs = np.float32(10000.0) ** (np.float32(-2.0) * np.arange(D // 2, dtype=np.float32) / np.float32(D))
    theta = np.arange(W, dtype=np.float32)[:, None] * freqs[None, :].astype(np.float32)
    cos, sin = np.cos(theta).astype(np.float32), np.sin(theta).astype(np.float32)
    c[:, C_COS:C_SIN] = np.repeat(cos, 2, axis=1)[p % W]
    c[:, C_SIN:C_MASK] = (np.repeat(sin, 2, axis=1) * np.tile([-1.0, 1.0], D // 2))[p % W]
    c[:, C_MASK:C_ROW] = np.where(np.arange(W)[None, :] <= (p % W)[:, None], 0.0, NEG)
    q = np.arange(32)
    c[:, C_ROW:C_SELC] = (p[:, None] % 64) == (32 * (q // 16) + q % 16)[None, :]
    for pr in range(E // 2):
        for e2 in range(2):
            rows = [r for r in range(2 * E) if r % E == 2 * pr + e2]
            c[rows, C_SELC + pr * P + 64 * e2:C_SELC + pr * P + 64 * e2 + 64] = 1.0
    for pair in range(NPAIR):
        for h2 in range(2):
            c[64 * h2:64 * h2 + 64, C_ONES + pair * 32 + 2 * pair + h2] = 1.0
    c[:, C_IDX:C_END] = (E - np.arange(E))[None, :]
    rot = np.zeros((P, W, P), np.float32)
    for h2 in range(2):
        for i in range(D // 2):
            a, b = 64 * h2 + 2 * i, 64 * h2 + 2 * i + 1
            rot[a, :, a], rot[b, :, b] = cos[:, i], cos[:, i]
            rot[b, :, a], rot[a, :, b] = -sin[:, i], sin[:, i]
    return c, rot.reshape(P, W * P)


def pe_order():
    jobs = []

    def add(region, *key):
        jobs.append((key, region))

    turn = [0]

    def add01(*key):
        add("P%d" % (turn[0] % 2), *key)
        turn[0] += 1

    def squares(hf, pairs):
        for p in pairs:
            add("", "squares", hf, p)

    def attention(hf, extra, between={}):
        for T in range(NT + 4):
            if T < NT:
                add01("S", hf, T)
            if 3 <= T < NT + 3:
                add("B4", "PT", hf, T - 3)
            for f in between.get(T, []):
                f()
            if T > NT:
                add01("PV", hf, T - 4)
            elif T >= 4:
                add("P2", "PV", hf, T - 4)
            for f in extra.get(T, []):
                f()

    def one(region, *key):
        return lambda: add(region, *key)

    add("B5", "score", 0)
    add("P2", "wb", 0, 0)
    add("P0", "wb", 0, 1)
    add("B4", "hT", 0)
    add("P2", "wb", 0, 2)
    add("B5", "xT", 0)
    add("P2", "wb", 0, 3)
    turn[0] = 1
    add01("A", 0, 0, 0)
    add("B4", "hT", 1)
    add("B5", "score", 1)
    add01("A", 0, 0, 1)
    add("P2", "kv", 0)
    add01("A", 0, 0, 2)
    add01("A", 0, 0, 3)
    add("B4", "xT", 1)
    add("P2", "kv", 1)
    add01("A", 0, 1, 0)
    add01("A", 0, 1, 1)
    add01("A", 0, 1, 2)
    add("P2", "wb", 1, 0)
    add01("A", 0, 1, 3)
    for k in range(8):
        add01("D", 0, k)
        if k == 0:
            add("B5", "ss", 0)
            squares(0, range(4))
        if k == 1:
            add("P2", "wb", 1, 1)
        if k == 3:
            squares(0, range(4, 8))
            add("P2", "wb", 1, 2)
        if k == 4:
            add("B4", "ssT", 0)
        if k == 5:
            add("P2", "wb", 1, 3)
    add("P2", "KT", 0)
    add("B5", "hT", 2)
    add("B4", "hT", 3)
    attention(0, {2: [one("B5", "xT", 2)], 3: [one("B5", "xT", 3)], 4: [one("B5", "kv", 2)], 5: [one("B5", "kv", 3)],
                  8: [one("B5", "OP", 0)], 9: [lambda: add01("A", 1, 0, 0), lambda: add01("A", 1, 0, 1)],
                  10: [lambda: add01("A", 1, 0, 2)], 11: [lambda: add01("A", 1, 0, 3), one("B4", "yT", 0)]})
    add("B5", "OP", 1)
    for q in range(4):
        add01("A", 1, 1, q)
        if q == 0:
            add("B4", "yT", 1)
    add("P2", "KT", 1)
    for k in range(8):
        add01("D", 1, k)
        if k == 0:
            add("B5", "ss", 1)
            squares(1, range(4))
        if k == 2:
            squares(1, range(4, 8))
        if k == 3:
            add("B4", "ssT", 1)
        if k == 4:
            add("P2", "x2T", 0)
        if k == 6:
            add("B5", "lg", 0)
    add01("L1", 0, 0)
    add01("L1", 0, 1)
    add("P2", "L1", 0, 2)
    attention(1, {0: [one("P2", "L1", 0, 3)], 1: [one("P2", "cT", 0), one("P2", "cb", 0, 0)],
                  2: [one("P2", "cb", 0, 1)], 3: [one("P2", "cb", 0, 2)], 4: [one("P2", "cb", 0, 3)],
                  5: [one("B5", "L2", 0)], 6: [one("B4", "zT", 0)],
                  7: [one("B5", "OP", 2)], 10: [one("B5", "x2T", 1)], 11: [one("B5", "lg", 1)]},
              {8: [one("B4", "yT", 2)]})
    add("B5", "OP", 3)
    add("B4", "yT", 3)
    for i in range(2):
        add01("L1", 1, i)
    add("P2", "cT", 1)
    add("P2", "cb", 1, 0)
    add("B5", "x2T", 2)
    add("P2", "cb", 1, 1)
    add("B4", "lg", 2)
    for i in range(2):
        add01("L1", 2, i)
    add("B5", "L2", 1)
    add("P2", "cT", 2)
    add("P2", "cb", 2, 0)
    add("B4", "zT", 1)
    add("P2", "cb", 2, 1)
    add("B5", "L2", 2)
    add("B4", "zT", 2)
    return jobs


def audio_tower(nc, x, tok_w_t, tok_b, wq_t, wkv_t, wo_t, q_norm_w, k_norm_w, router_t, w1_t, b1_t, w2, b2,
                const, rot, out):
    jobs = pe_order()
    region_of, use_of, uses = {}, {}, {}
    for key, region in jobs:
        uses[region] = uses.get(region, 0) + 1
        region_of[key], use_of[key] = region, uses[region]

    with ExitStack() as ctx:
        def sb(name, shape, dt=F32):
            return ctx.enter_context(nc.sbuf_tensor(name, shape, dt))

        def sem(name):
            return ctx.enter_context(nc.semaphore(name))

        ps = {r: ctx.enter_context(nc.psum_tensor("ps_" + r, [P, 1024], F32)) for r in ("P0", "P1", "P2")}
        ps |= {r: ctx.enter_context(nc.psum_tensor("ps_" + r, [P, 512], F32)) for r in ("B4", "B5")}
        filled = {r: sem("filled_" + r) for r in ps}
        freed = {r: sem("freed_" + r) for r in ps}

        qr_sb = sb("qr_sb", [P, RB, NPAIR, W])
        raw = qr_sb[:, :, :, :].rearrange("p b a t -> p (b a t)")
        wq_raw, wkv_raw, w1_raw, router_raw = (raw[:, a:b] for a, b in ((0, 1024), (1024, 1152), (1152, 1664), (1664, 1672)))
        cst = sb("cst", [P, C_END])
        ident = cst[:, C_ID:C_COS]
        rot_sb = sb("rot_sb", [P, W, P])
        w2_sb = sb("w2_sb", [P, E // 2, D])
        b1_sb = sb("b1_sb", [P, E // 2])
        b2_sb = sb("b2_sb", [P, D])
        norm_w = sb("norm_w", [P, 2, D])
        key_gain = sb("key_gain", [P, D])
        tokb_sb = sb("tokb_sb", [P, 1])
        wz = sb("wz", [P, 64])
        wqT = sb("wqT", [P, 2, H * D], F32R)
        wkvT = sb("wkvT", [P, 2, P], F32R)
        routerT = sb("routerT", [P, 2, E], F32R)
        w1s = sb("w1s", [P, 2, E * D], F32R)
        woT = sb("woT", [P, NPAIR, D])
        row_sel = sb("row_sel", [P, 32, D], F32R)
        expert_sel = sb("expert_sel", [P, E // 2, P], F32R)

        x_sb = sb("x_sb", [P, HALVES * NJ, TIME])
        score_sb = sb("score_sb", [P, TIME])
        pool_w = sb("pool_w", [P, TIME])
        pool_ws = sb("pool_ws", [P, HALVES, TIME], F32R)
        win_stat = sb("win_stat", [P, 3, W])
        prod = sb("prod", [P, 2, 4 * TIME])
        pooledT = sb("pooledT", [P, NJ * W])
        after_x = x_sb[:, :, :].rearrange("p j t -> p (j t)")
        value_block = after_x[:, 0:RB * P].rearrange("p (b m) -> p b m", b=RB)
        key_block = after_x[:, 4096:4096 + (RB + 1) * 2 * W].rearrange("p (b s) -> p b s", b=RB + 1)
        y_sb = after_x[:, 6208:6720]
        rq_stat = after_x[:, 6720:7104].rearrange("p (a n) -> p a n", a=3)
        after_prod = prod[:, :, :].rearrange("p r n -> p (r n)")
        probT = after_prod[:, 0:1024].rearrange("p (r q g n) -> p r q g n", r=2, q=2, g=2)
        h2_sb = after_prod[:, 1024:2048].rearrange("p (n f) -> p n f", f=D)
        gateT = row_sel[:, 0:16, :].rearrange("p a f -> p (a f)")
        h_sb = sb("h_sb", [P, HALVES * NT, D])
        ktmp = sb("ktmp", [P, 2, NT, D])
        key_tmp = sb("key_tmp", [P, NT, D])
        ln_sb = sb("ln_sb", [P, NT, 2, D])
        stat = sb("stat", [P, 8, NT])
        xs = sb("xs", [P, TOK], F32R)
        kv_sb = sb("kv_sb", [P, NT, P])
        kn = sb("kn", [P, NT, 2, D])
        q_sb = sb("q_sb", [P, NPAIR, TOK])
        o_sb = q_sb
        sq_sb = sb("sq_sb", [P, SQ_RING, TOK])
        ssq_sb = sb("ssq_sb", [P, 256])
        prob = sq_sb[:, 0:2, :].rearrange("p q n -> p (q n)").rearrange("p (r g j h s) -> p r g j h s", r=PROB_RING, g=2, j=4, h=2)
        rq = sb("rq", [P, HALVES, NT, 2, 4, 2])
        row_stat = sb("row_stat", [P, PROB_RING, 3, 16])
        ln2_sb = ln_sb
        xs2 = xs
        rt = sb("rt", [P, 8, NT, E])
        r1 = sb("r1", [P, 6, NT])
        gate = sb("gate", [P, HALVES * NT, 2 * E], F32R)
        hid = rot_sb[:, :, :].rearrange("p t m -> p (t m)").rearrange("p (r n) -> p r n", r=E // 2)
        z_sb = y_sb

        s_cst, s_rot, s_tokw, s_wq, s_wsm, s_w1, s_wff, s_wo, s_out = (
            sem(n) for n in ("cst_in", "rot_in", "tokw_in", "wq_in", "wsmall_in", "w1_in", "wffn_in", "wo_in", "out_stored"))
        s_x = [[sem(f"x_in{h}{g}") for g in range(2)] for h in range(HALVES)]
        names = ("wz_zero zeroed weights_hi weights_ready selectors dve_link score_shift pool_exp pool_w_ready pooled pooled_p "
                 "ln_ready xs_hi kn_ready values_in q_squared q_squared_p squares_used keys_rotated pool_link scales_moved scores_shifted logits_ready prob_exp "
                 "prob_sums prob_ready ln2_ready xs2_hi gate_exp gate_ready").split()
        S = {n: sem(n) for n in names}
        block = ctx.enter_context(nc.Block())

        def wait_filled(eng, *key):
            r = region_of[key]
            eng.wait_ge(filled[r], use_of[key])
            return ps[r]

        def is_freed(*key):
            return freed[region_of[key]]

        def wait_freed(eng, *key):
            eng.wait_ge(freed[region_of[key]], use_of[key])

        def rotated(k):
            return qr_sb[:, :, :, 4 * k:4 * k + 4].rearrange("p b a t -> p t a b")

        def square_slot_free(eng, hf, p):
            if p >= SQ_RING:
                eng.wait_ge(S["squares_used"], (NPAIR - 1) * hf + p - SQ_RING + 1)
            elif hf:
                wait_filled(eng, "PT", 0, NT - 1)

        @block.sync
        def _(sp):
            xv = x.rearrange("(j c) f t -> (c f) j t", c=2)
            for hf in range(HALVES):
                if hf:
                    sp.wait_ge(s_x[0][0], 16)
                for g in range(2):
                    j = NJ * hf + 8 * g
                    sp.dma_start(x_sb[:, j:j + 8, :], xv[:, j:j + 8, :]).then_inc(s_x[hf][g], 16)
            sp.dma_start(w1_raw[0:64, :], w1_t).then_inc(s_w1, 16)
            sp.dma_start(w1_raw[64:128, :], w1_t).then_inc(s_w1, 16)
            sp.dma_start(rot_sb[:, :, :], rot.rearrange("p (t m) -> p t m", t=W)).then_inc(s_rot, 16)
            sp.dma_start(w2_sb[:, :, :], w2.rearrange("(a e) f m -> (e f) a m", e=2)).then_inc(s_wff, 16)
            sp.dma_start(b1_sb[:, :], b1_t).then_inc(s_wff, 16)
            sp.dma_start(woT[:, :, :], wo_t.rearrange("p (a m) -> p a m", a=NPAIR)).then_inc(s_wo, 16)
            sp.wait_ge(S["zeroed"], 1)
            sp.dma_start(b2_sb[0:E, :], b2).then_inc(s_wff, 16)
            sp.dma_start(b2_sb[E:2 * E, :], b2).then_inc(s_wff, 16)
            ov = out.rearrange("(J j c) w f -> c j w J f", c=2, j=4)
            n = 0
            for s, (t0, nt) in enumerate(SEG):
                wait_freed(sp, "zT", s)
                r = h2_sb[:, t0:t0 + nt, :].rearrange("p (J c) f -> p c J f", c=2)
                for J in range(nt // 2):
                    for c in range(2):
                        sp.dma_start(ov[c, :, :, t0 // 2 + J, :], r[:, c, J, :]).then_inc(s_out, 16)
                        n += 16
            sp.wait_ge(s_out, n)

        @block.gpsimd
        def _(pool):
            def rows(n):
                return prob[:, n % PROB_RING, :, :, :, :].rearrange("p g j h s -> p (g j h) s")

            def scale(hf, T):
                n = NT * hf + T
                pool.wait_ge(S["scales_moved"], hf + 1)
                pool.wait_ge(S["scores_shifted"], n + 1)
                r = rq[:, hf, T, :, :, :].rearrange("p g j h -> p (g j h)")
                nc.gpsimd.tensor_tensor(rows(n), rows(n), r.unsqueeze(2).to_broadcast([P, 16, W]),
                                        ALU.mult).then_inc(S["logits_ready"], 1)

            def normalise(hf, T):
                n = NT * hf + T
                pool.wait_ge(S["prob_sums"], n + 1)
                nc.gpsimd.tensor_tensor(rows(n), rows(n), row_stat[:, n % PROB_RING, 2, :].unsqueeze(2).to_broadcast([P, 16, W]),
                                        ALU.mult).then_inc(S["prob_ready"], 1)

            nc.gpsimd.memset(wz[:, :], 0.0).then_inc(S["wz_zero"], 1)
            nc.gpsimd.memset(b2_sb[:, :], 0.0).then_inc(S["zeroed"], 1)
            def squares(hf, p):
                wait_freed(pool, "A", hf, 0, p // 2)
                square_slot_free(pool, hf, p)
                nc.gpsimd.tensor_tensor(sq_sb[:, p % SQ_RING, 0:512], q_sb[:, p, 0:512], q_sb[:, p, 0:512],
                                        ALU.mult).then_inc(S["q_squared_p"], 1)

            steps = [0]

            def link(ins):
                steps[0] += 1
                ins.then_inc(S["pool_link"], 1)
                pool.wait_ge(S["pool_link"], steps[0])

            def rope(hf):
                wait_freed(pool, "kv", 2 * hf)
                wait_freed(pool, "kv", 2 * hf + 1)
                mul = nc.gpsimd.tensor_tensor
                k, b = kv_sb[:, :, 0:D], key_tmp[:, :, :]
                cos, sin = (cst[:, o:o + D].unsqueeze(1).to_broadcast([P, NT, D]) for o in (C_COS, C_SIN))
                kp, bp, sp_ = (a.rearrange("p n (i c) -> p n i c", c=2) for a in (k, b, sin))
                for c in range(2):
                    link(mul(bp[:, :, :, c], kp[:, :, :, 1 - c], sp_[:, :, :, c], ALU.mult))
                link(mul(k, k, cos, ALU.mult))
                link(mul(k, k, b, ALU.add))
                mul(b, k, k, ALU.mult).then_inc(S["keys_rotated"], 1)

            def lo_part(parts, raw_w):
                nc.gpsimd.tensor_tensor(parts[:, 1, :], raw_w, parts[:, 0, :].bitcast(F32), ALU.subtract)\
                    .then_inc(S["weights_ready"], 1)

            def window_sum(hf, i):
                n = 4 * hf + i
                wait_freed(pool, "wb", hf, i)
                v = prod[:, n % 2, :].rearrange("p (w k) -> p w k", k=K)
                add_ = nc.gpsimd.tensor_tensor
                link(add_(v[:, :, 0:4], v[:, :, 0:4], v[:, :, 4:8], ALU.add))
                link(add_(v[:, :, 0:2], v[:, :, 0:2], v[:, :, 2:4], ALU.add))
                if hf:
                    wait_filled(pool, "hT", 1)
                add_(pooledT[:, 4 * W * i:4 * W * (i + 1)].unsqueeze(2), v[:, :, 0:1], v[:, :, 1:2], ALU.add)\
                    .then_inc(S["pooled_p"], 1)

            for n, (parts, raw_w) in enumerate(((wqT, wq_raw), (wkvT, wkv_raw), (routerT, router_raw))):
                pool.wait_ge(S["weights_hi"], n + 1)
                lo_part(parts, raw_w)
            window_sum(0, 2)
            pool.wait_ge(s_w1, 32)
            link(nc.gpsimd.tensor_copy(w1s[:, 0, :], w1_raw))
            lo_part(w1s, w1_raw)
            pool.wait_ge(s_cst, 16)
            for p in range(4):
                squares(0, p)
            wait_freed(pool, "wb", 0, 3)
            nc.gpsimd.memset(value_block[:, :, :], 0.0).then_inc(S["zeroed"], 1)
            rope(0)
            for p in range(4, NPAIR):
                squares(0, p)
            window_sum(1, 1)
            wait_freed(pool, "wb", 1, 2)
            nc.gpsimd.memset(key_block[:, :, :], 0.0).then_inc(S["zeroed"], 1)
            window_sum(1, 2)
            for hf in range(HALVES):
                if hf:
                    for p in range(NPAIR):
                        squares(hf, p)
                for T in range(NT + 1):
                    if T < NT:
                        scale(hf, T)
                    if T >= 1:
                        normalise(hf, T - 1)
                if hf == 0:
                    rope(1)
                    wait_filled(pool, "wb", 1, 3)
                    nc.gpsimd.memset(gateT[:, :].bitcast(F32), 0.0).then_inc(S["zeroed"], 1)

        @block.scalar
        def _(act):
            act.wait_ge(S["wz_zero"], 1)
            act.dma_start(wz[0:64, 30:31], tok_w_t).then_inc(s_tokw, 16)
            act.dma_start(wz[64:128, 31:32], tok_w_t).then_inc(s_tokw, 16)
            act.dma_start(tokb_sb[:, :], tok_b.rearrange("(a o) -> a o", a=1).to_broadcast([P, 1])).then_inc(s_tokw, 16)
            act.dma_start(cst[:, :], const).then_inc(s_cst, 16)
            for c in range(2):
                r = slice(D * c, D * c + D)
                act.dma_start(wq_raw[r, :], wq_t).then_inc(s_wq, 16)
                act.dma_start(wkv_raw[r, :], wkv_t).then_inc(s_wsm, 16)
                act.dma_start(router_raw[r, :], router_t).then_inc(s_wsm, 16)
            act.dma_start(norm_w[:, 0, :], q_norm_w.rearrange("(a d) -> a d", a=1).to_broadcast([P, D])).then_inc(s_wsm, 16)
            act.dma_start(norm_w[:, 1, :], k_norm_w.rearrange("(a d) -> a d", a=1).to_broadcast([P, D])).then_inc(s_wsm, 16)

            def copy(o, i):
                return nc.scalar.activation(o, i, ACT.Copy)

            act.wait_ge(s_wq, 32)
            copy(wqT[:, 0, :], wq_raw).then_inc(S["weights_hi"], 1)

            def pool_exp(hf):
                r = slice(64 * hf, 64 * hf + 64)
                act.wait_ge(S["score_shift"], hf + 1)
                nc.scalar.activation(pool_w[r, :], score_sb[r, :], ACT.Exp).then_inc(S["pool_exp"], 1)

            def h_out(q):
                t = wait_filled(act, "hT", q)
                copy(h_sb[:, 4 * q:4 * q + 4, :], t[:, 0:256].rearrange("p (n f) -> p n f", f=D)).then_inc(is_freed("hT", q), 1)

            def xs_hi(q):
                t = wait_filled(act, "xT", q)
                if q >= 2:
                    wait_filled(act, "A", 0, 1, 3)
                    wait_filled(act, "kv", 1)
                copy(xs[:, 512 * (q % 2):512 * (q % 2) + 512], t[:, :]).then_inc(S["xs_hi"], 1)

            def kv_out(q):
                t = wait_filled(act, "kv", q)
                if q == 2:
                    act.wait_ge(S["values_in"], 4)
                copy(kv_sb[:, 4 * (q % 2):4 * (q % 2) + 4, :], t[:, 0:512].rearrange("p (n f) -> p n f", f=P))\
                    .then_inc(is_freed("kv", q), 1)

            def keys_in(hf):
                t = wait_filled(act, "KT", hf)
                act.wait_ge(S["zeroed"], 3)
                if hf:
                    wait_filled(act, "S", 0, NT - 1)
                for h2 in range(2):
                    r = slice(64 * h2, 64 * h2 + 64)
                    i = copy(key_block[r, 0:RB, W * h2:W * h2 + W], t[r, :].rearrange("p (b s) -> p b s", s=W))
                i.then_inc(is_freed("KT", hf), 1)

            def q_out(hf, c, q):
                t = wait_filled(act, "A", hf, c, q)
                if hf and q == 0:
                    wait_filled(act, "OP", c)
                copy(q_sb[:, 2 * q:2 * q + 2, 512 * c:512 * c + 512], t[:, :].rearrange("p (a n) -> p a n", a=2))\
                    .then_inc(is_freed("A", hf, c, q), 1)

            def q_square(hf, p):
                wait_freed(act, "A", hf, 1, p // 2)
                square_slot_free(act, hf, p)
                nc.scalar.activation(sq_sb[:, p % SQ_RING, 512:1024], q_sb[:, p, 512:1024],
                                     ACT.Square).then_inc(S["q_squared"], 1)

            def qr_out(hf, k):
                t = wait_filled(act, "D", hf, k)
                if k == 0 and hf:
                    wait_filled(act, "S", 0, NT - 1)
                elif k == 0:
                    act.wait_ge(S["weights_ready"], 4)
                copy(rotated(k), t[:, :].rearrange("p (t a b) -> p t a b", t=4, a=NPAIR)).then_inc(is_freed("D", hf, k), 1)

            def values_in(hf, j4):
                wait_freed(act, "kv", 2 * hf)
                wait_freed(act, "kv", 2 * hf + 1)
                if hf:
                    wait_filled(act, "PV", 0, NT - 1)
                else:
                    act.wait_ge(S["zeroed"], 2)
                vb = value_block[:, :, :].rearrange("p (n j) m -> p n j m", j=4)
                for h2 in range(2):
                    q = 2 * (j4 % 2) + h2
                    i = copy(vb[32 * q:32 * q + 32, :, j4, D * h2:D * h2 + D], kv_sb[32 * j4:32 * j4 + 32, :, D:2 * D])
                i.then_inc(S["values_in"], 1)

            def exp_out(hf, T):
                n = NT * hf + T
                act.wait_ge(S["logits_ready"], n + 1)
                e = prob[:, n % PROB_RING, :, :, :, :].rearrange("p g j h s -> p (g j h s)")
                nc.scalar.activation(e, e, ACT.Exp).then_inc(S["prob_exp"], 1)

            def attended_out(hf, T):
                t = wait_filled(act, "PV", hf, T)
                if T == 0:
                    wait_filled(act, "D", hf, 7)
                copy(o_sb[:, :, P * T:P * T + P].rearrange("p a (j t) -> p j a t", j=4),
                     t[:, :].rearrange("p (j a t) -> p j a t", j=4, a=NPAIR)).then_inc(is_freed("PV", hf, T), 1)

            def probT_out(hf, T):
                t = wait_filled(act, "PT", hf, T)
                copy(probT[:, T % 2, :, :, :], t[:, :].rearrange("p (g r n) -> p r g n", g=2, r=2))\
                    .then_inc(is_freed("PT", hf, T), 1)

            def attn(hf, extra):
                for T in range(NT + 4):
                    if 3 <= T < NT + 3:
                        probT_out(hf, T - 3)
                    if T >= 4:
                        attended_out(hf, T - 4)
                    if T < NT:
                        exp_out(hf, T)
                    for f in extra.get(T, []):
                        f()

            def y_out(q):
                t = wait_filled(act, "OP", q)
                if q == 2:
                    wait_filled(act, "zT", 0)
                o = 256 * (q % 2)
                copy(y_sb[:, o:o + 256], t[:, 0:256]).then_inc(is_freed("OP", q), 1)

            def xs2_hi(s):
                t0, nt = SEG[s]
                t = wait_filled(act, "x2T", s)
                if s == 0:
                    wait_filled(act, "A", 1, 1, 3)
                    wait_filled(act, "kv", 3)
                elif s == 1:
                    wait_filled(act, "L1", 0, 3)
                    wait_filled(act, "lg", 0)
                copy(xs2[:, P * (t0 % NT):P * (t0 % NT + nt)], t[:, 0:P * nt]).then_inc(S["xs2_hi"], 1)

            def gate_exp(s):
                nt = SEG[s][1]
                wait_freed(act, "lg", s)
                nc.scalar.activation(rt[:, 0, 0:nt, :], rt[:, 0, 0:nt, :], ACT.Exp).then_inc(S["gate_exp"], 1)

            def gateT_out(s):
                t0, nt = SEG[s]
                t = wait_filled(act, "cT", s)
                if s:
                    wait_filled(act, "L2", 0)
                act.wait_ge(S["zeroed"], 4)
                copy(gateT[0:2 * E, P * (t0 % NT):P * (t0 % NT + nt)], t[0:2 * E, 0:P * nt]).then_inc(is_freed("cT", s), 1)

            def gelu(s):
                t0, nt = SEG[s]
                if s == 0:
                    act.wait_ge(s_wff, 64)
                wait_filled(act, *(("L2", 0) if s else ("D", 1, 7)))
                for i in range(nt // 2):
                    t = wait_filled(act, "L1", s, i)
                    n = 8 // nt
                    for a in range(n):
                        pr = n * i + a
                        ins = nc.scalar.activation(hid[:, pr, P * (t0 % NT):P * (t0 % NT + nt)],
                                                   t[:, P * nt * a:P * nt * (a + 1)], ACT.Gelu, bias=b1_sb[:, pr:pr + 1])
                    ins.then_inc(is_freed("L1", s, i), 1)

            def z_out(s):
                n = 64 * SEG[s][1]
                o = 256 * (s == 2)
                t = wait_filled(act, "L2", s)
                wait_filled(act, "yT", s + 1)
                copy(z_sb[:, o:o + n], t[:, 0:n]).then_inc(is_freed("L2", s), 1)

            def squares_and_rotated(hf):
                qr_out(hf, 0)
                for p in range(4, 8):
                    q_square(hf, p)
                qr_out(hf, 1)
                if hf:
                    keys_in(hf)
                qr_out(hf, 2)
                qr_out(hf, 3)

            def queries_and_squares(hf, c1):
                for q in c1:
                    q_out(hf, 1, q)
                    if q < 2:
                        q_square(hf, 2 * q)
                        q_square(hf, 2 * q + 1)

            pool_exp(0)
            act.wait_ge(s_wsm, 16 * 6)
            copy(wkvT[:, 0, :], wkv_raw).then_inc(S["weights_hi"], 1)
            copy(routerT[:, 0, :], router_raw).then_inc(S["weights_hi"], 1)
            h_out(0)
            xs_hi(0)
            q_out(0, 0, 0)
            h_out(1)
            q_out(0, 0, 1)
            kv_out(0)
            q_out(0, 0, 2)
            q_out(0, 0, 3)
            xs_hi(1)
            kv_out(1)
            pool_exp(1)
            for q in range(4):
                q_out(0, 1, q)
            for p in range(4):
                q_square(0, p)
            squares_and_rotated(0)
            for k in range(4, 8):
                values_in(0, k - 4)
                qr_out(0, k)
            h_out(2)
            h_out(3)
            keys_in(0)
            attn(0, {2: [lambda: xs_hi(2)], 3: [lambda: xs_hi(3)], 4: [lambda: kv_out(2)], 5: [lambda: kv_out(3)], 8: [lambda: y_out(0)],
                     9: [lambda: q_out(1, 0, 0), lambda: q_out(1, 0, 1)], 10: [lambda: q_out(1, 0, 2)],
                     11: [lambda: q_out(1, 0, 3)]})
            y_out(1)
            queries_and_squares(1, range(4))
            squares_and_rotated(1)
            qr_out(1, 4)
            xs2_hi(0)
            qr_out(1, 5)
            values_in(1, 0)
            qr_out(1, 6)
            values_in(1, 1)
            gate_exp(0)
            qr_out(1, 7)
            gelu(0)
            attn(1, {0: [lambda: gateT_out(0)], 1: [lambda: values_in(1, 2)], 2: [lambda: values_in(1, 3)], 5: [lambda: z_out(0)], 7: [lambda: y_out(2)], 10: [lambda: xs2_hi(1)], 11: [lambda: gate_exp(1)]})
            y_out(3)
            gelu(1)
            gateT_out(1)
            xs2_hi(2)
            gate_exp(2)
            gelu(2)
            z_out(1)
            gateT_out(2)
            z_out(2)

        @block.vector
        def _(dve):
            chain = [0]

            def link(ins):
                chain[0] += 1
                ins.then_inc(S["dve_link"], 1)
                dve.wait_ge(S["dve_link"], chain[0])

            tt, ts, red, stt = (nc.vector.tensor_tensor, nc.vector.tensor_scalar, nc.vector.tensor_reduce,
                                nc.vector.scalar_tensor_tensor)

            def bc(a, n):
                return a.unsqueeze(len(a.shape)).to_broadcast([*a.shape, n])

            def rsqrt(y, v, t):
                link(ts(t.bitcast(I32), v.bitcast(I32), 1, None, ALU.logical_shift_right))
                link(ts(y.bitcast(I32), t.bitcast(I32), -1.0, float(RSQRT_MAGIC), ALU.mult, ALU.add))
                for step in range(3):
                    link(tt(t, y, y, ALU.mult))
                    link(stt(out=t, in0=t, scalar=-0.5, in1=v, op0=ALU.mult, op1=ALU.mult))
                    last = stt(out=y, in0=t, scalar=1.5, in1=y, op0=ALU.add, op1=ALU.mult)
                    if step < 2:
                        link(last)
                return last

            dve.wait_ge(s_cst, 16)
            nc.vector.tensor_copy(row_sel[:, :, :], bc(cst[:, C_ROW:C_SELC], D)).then_inc(S["selectors"], 1)
            nc.vector.tensor_copy(expert_sel[:, :, :], cst[:, C_SELC:C_ONES].rearrange("p (a n) -> p a n", n=P))\
                .then_inc(S["selectors"], 1)

            def key_gains():
                dve.wait_ge(s_wsm, 16 * 6)
                link(stt(out=key_gain[:, :], in0=norm_w[:, 0, :], scalar=float(D) ** -0.5, in1=norm_w[:, 1, :],
                         op0=ALU.mult, op1=ALU.mult))

            def pool_softmax(hf):
                r = slice(64 * hf, 64 * hf + 64)
                t = wait_filled(dve, "score", hf)
                sc, pw = score_sb[r, :], pool_w[r, :]
                mx, sm, inv = (win_stat[r, i, :] for i in range(3))
                dve.wait_ge(s_tokw, 48)
                ts(sc, t[r, 0:TIME], tokb_sb[r, :], None, ALU.add).then_inc(is_freed("score", hf), 1)
                wait_freed(dve, "score", hf)
                v = sc.rearrange("p (w k) -> p w k", k=K)
                link(red(mx, v, AX, ALU.max))
                tt(v, v, bc(mx, K), ALU.subtract).then_inc(S["score_shift"], 1)
                dve.wait_ge(S["pool_exp"], hf + 1)
                v = pw.rearrange("p (w k) -> p w k", k=K)
                link(red(sm, v, AX, ALU.add))
                link(nc.vector.reciprocal(inv, sm))
                link(tt(v, v, bc(inv, K), ALU.mult))
                other = slice(64 - 64 * hf, 128 - 64 * hf)
                link(nc.vector.tensor_copy(pool_ws[r, hf, :], pw))
                tt(pool_ws[other, hf, :], pw, pool_ws[r, hf, :].bitcast(F32), ALU.subtract)\
                    .then_inc(S["pool_w_ready"], 1)

            def pool_sum(hf, i):
                n = 4 * hf + i
                t = wait_filled(dve, "wb", hf, i)
                j = NJ * hf + 4 * i
                pr = prod[:, n % 2, :]
                sent = [m for m in range(n - 1) if m % 4 in GPSIMD_SUMS[m // 4]]
                if sent:
                    dve.wait_ge(S["pooled_p"], len(sent))
                tt(pr, t[:, :], x_sb[:, j:j + 4, :].rearrange("p j t -> p (j t)"), ALU.mult)\
                    .then_inc(is_freed("wb", hf, i), 1)
                wait_freed(dve, "wb", hf, i)
                if hf and i == 0:
                    wait_filled(dve, "hT", 1)
                if i in GPSIMD_SUMS[hf]:
                    return
                red(pooledT[:, 4 * W * i:4 * W * (i + 1)], pr.rearrange("p (w k) -> p w k", k=K), AX, ALU.add)\
                    .then_inc(S["pooled"], 1)

            def layernorm(o, h, nt):
                sm, ss, v, y, t = (stat[:, i, 0:nt] for i in range(5))
                dev, sqd = ktmp[:, 0, 0:nt, :], ktmp[:, 1, 0:nt, :]
                link(red(sm, h, AX, ALU.add))
                link(stt(out=dev, in0=bc(sm, D), scalar=-1.0 / D, in1=h, op0=ALU.mult, op1=ALU.add))
                link(tt(sqd, dev, dev, ALU.mult))
                link(red(ss, sqd, AX, ALU.add))
                link(ts(v, ss, 1.0 / D, EPS_LN, ALU.mult, ALU.add))
                link(rsqrt(y, v, t))
                d2 = dev.unsqueeze(2).to_broadcast([P, nt, 2, D])
                y2 = y.unsqueeze(2).unsqueeze(3).to_broadcast([P, nt, 2, D])
                return tt(o, d2, y2, ALU.mult)

            def ln1(q, nq):
                for i in range(q, q + nq):
                    wait_freed(dve, "hT", i)
                if q == 2:
                    wait_filled(dve, "xT", 1)
                c = 4 * (q % 2)
                layernorm(ln_sb[:, c:c + 4 * nq, :, :], h_sb[:, 4 * q:4 * (q + nq), :], 4 * nq).then_inc(S["ln_ready"], nq)

            def xs_lo(q):
                t = wait_filled(dve, "xT", q)
                dve.wait_ge(S["xs_hi"], q + 1)
                o = xs[64:128, 512 * (q % 2):512 * (q % 2) + 512]
                tt(o, t[64:128, :], o.bitcast(F32), ALU.subtract).then_inc(is_freed("xT", q), 1)

            def keys(hf):
                dve.wait_ge(S["keys_rotated"], hf + 1)
                ss, v, y, t = (stat[:, i, 0:NT] for i in range(4))
                link(red(ss, key_tmp[:, :, :], AX, ALU.add))
                link(ts(v, ss, 1.0 / D, EPS_RMS, ALU.mult, ALU.add))
                link(rsqrt(y, v, t))
                a = ktmp[:, 0, :, :]
                link(tt(a, kv_sb[:, :, 0:D], bc(y, D), ALU.mult))
                if hf:
                    wait_filled(dve, "KT", 0)
                g = key_gain[:, :].unsqueeze(1).unsqueeze(1).to_broadcast([P, NT, 2, D])
                tt(kn[:, :, :, :], a.unsqueeze(2).to_broadcast([P, NT, 2, D]), g, ALU.mult)\
                    .then_inc(S["kn_ready"], 1)

            def ssq_out(hf):
                t = wait_filled(dve, "ss", hf)
                nc.vector.tensor_copy(ssq_sb[:, :], t[:, 0:256]).then_inc(is_freed("ss", hf), 1)

            def query_scales(hf):
                t = wait_filled(dve, "ssT", hf)
                v, y, tmp = (rq_stat[:, i, :] for i in range(3))
                tv = t[:, 0:256].rearrange("p (i c h) -> p c i h", i=2, c=4)[:, :, :, 0:H]
                ts(v.rearrange("p (c i h) -> p c i h", c=4, i=2), tv, 1.0 / D, EPS_RMS, ALU.mult, ALU.add)\
                    .then_inc(is_freed("ssT", hf), 1)
                wait_freed(dve, "ssT", hf)
                link(rsqrt(y, v, tmp))
                yv = y.rearrange("p (n g a h) -> p n g a h", n=NT, g=2, a=4)
                for j4 in range(4):
                    for a in range(4):
                        i = nc.vector.tensor_copy(rq[32 * a:32 * a + 32, hf, :, :, j4, :],
                                                  yv[32 * j4:32 * j4 + 32, :, :, a, :])
                i.then_inc(S["scales_moved"], 1)

            def shift(hf, T):
                n = NT * hf + T
                t = wait_filled(dve, "S", hf, T)
                if n >= PROB_RING:
                    m = n - PROB_RING
                    wait_filled(dve, "PT", m // NT, m % NT)
                e16 = prob[:, n % PROB_RING, :, :, :, :].rearrange("p g j h s -> p (g j) h s")
                sv = t[:, :].rearrange("p (n x) -> p n x", x=P)[:, :, 0:2 * W].rearrange("p n (h s) -> p n h s", h=2)
                m = cst[:, C_MASK:C_ROW].unsqueeze(1).unsqueeze(1).to_broadcast([P, 8, 2, W])
                tt(e16, sv, m, ALU.add).then_inc(is_freed("S", hf, T), 1)
                wait_freed(dve, "S", hf, T)
                e = prob[:, n % PROB_RING, :, :, :, :].rearrange("p g j h s -> p (g j h) s")
                mx = row_stat[:, n % PROB_RING, 0, :]
                link(red(mx, e, AX, ALU.max))
                tt(e, e, bc(mx, W), ALU.subtract).then_inc(S["scores_shifted"], 1)

            def sums(hf, T):
                n = NT * hf + T
                dve.wait_ge(S["prob_exp"], n + 1)
                e = prob[:, n % PROB_RING, :, :, :, :].rearrange("p g j h s -> p (g j h) s")
                link(red(row_stat[:, n % PROB_RING, 1, :], e, AX, ALU.add))
                nc.vector.reciprocal(row_stat[:, n % PROB_RING, 2, :], row_stat[:, n % PROB_RING, 1, :])\
                    .then_inc(S["prob_sums"], 1)

            def attn(hf, extra):
                for T in range(NT + 1):
                    if T < NT:
                        shift(hf, T)
                    if T >= 1:
                        sums(hf, T - 1)
                    for f in extra.get(T, []):
                        f()

            def ln2(s):
                t0, nt = SEG[s]
                for q in range(t0 // 4, (t0 + nt) // 4):
                    t = wait_filled(dve, "yT", q)
                    tv = t[:, 0:256].rearrange("p (i c m) -> p c i m", c=2, m=D)
                    h, h2 = (b[:, 4 * q:4 * q + 4, :].rearrange("p (c i) m -> p c i m", c=2) for b in (h_sb, h2_sb))
                    tt(h2, tv, h, ALU.add).then_inc(is_freed("yT", q), 1)
                    wait_freed(dve, "yT", q)
                h2 = h2_sb[:, t0:t0 + nt, :]
                wait_filled(dve, *(("x2T", 0) if s else ("xT", 3)))
                o = ln2_sb[:, t0 % NT:t0 % NT + nt, :, :]
                layernorm(o, h2, nt).then_inc(S["ln2_ready"], 1)
                dve.wait_ge(S["ln2_ready"], s + 1)
                link(tt(h2, h2, o[:, :, 0, :], ALU.add))

            def xs2_lo(s):
                t0, nt = SEG[s]
                t = wait_filled(dve, "x2T", s)
                dve.wait_ge(S["xs2_hi"], s + 1)
                o = xs2[64:128, P * (t0 % NT):P * (t0 % NT + nt)]
                tt(o, t[64:128, 0:P * nt], o.bitcast(F32), ALU.subtract).then_inc(is_freed("x2T", s), 1)

            def router(s):
                nt = SEG[s][1]
                t = wait_filled(dve, "lg", s)
                lg = t[:, 0:nt * E].rearrange("p (n e) -> p n e", e=E)
                m0 = r1[:, 0, 0:nt]
                link(red(m0, lg, AX, ALU.max))
                tt(rt[:, 0, 0:nt, :], lg, bc(m0, E), ALU.subtract).then_inc(is_freed("lg", s), 1)

            def top2(s):
                t0, nt = SEG[s]
                p_, e1, o1, p2, e2, o2, cc = (rt[:, i, 0:nt, :] for i in range(7))
                sm, m1, m2, x1, dn = (r1[:, i, 0:nt] for i in range(1, 6))
                idx = cst[:, C_IDX:C_END].unsqueeze(1).to_broadcast([P, nt, E])
                dve.wait_ge(S["gate_exp"], s + 1)
                link(red(sm, p_, AX, ALU.add))
                link(nc.vector.reciprocal(dn, sm))
                link(tt(p_, p_, bc(dn, E), ALU.mult))

                def largest(q, m, eq, o):
                    link(red(m, q, AX, ALU.max))
                    link(tt(eq, q, bc(m, E), ALU.is_equal))
                    link(tt(eq, eq, idx, ALU.mult))
                    link(red(x1, eq, AX, ALU.max))
                    link(tt(o, eq, bc(x1, E), ALU.is_equal))

                largest(p_, m1, e1, o1)
                link(stt(out=p2, in0=o1, scalar=-4.0, in1=p_, op0=ALU.mult, op1=ALU.add))
                largest(p2, m2, e2, o2)
                link(tt(cc, o1, o2, ALU.add))
                link(tt(cc, cc, p_, ALU.mult))
                link(tt(sm, m1, m2, ALU.add))
                link(ts(sm, sm, 1e-12, None, ALU.max))
                link(nc.vector.reciprocal(dn, sm))
                link(tt(cc, cc, bc(dn, E), ALU.mult))
                g = gate[:, t0:t0 + nt, :]
                link(nc.vector.tensor_copy(g[:, :, 0:E], cc))
                tt(g[:, :, E:2 * E], cc, g[:, :, 0:E].bitcast(F32), ALU.subtract).then_inc(S["gate_ready"], 1)

            def gate_hidden(s, i):
                t0, nt = SEG[s]
                n = 8 // nt
                wait_freed(dve, "L1", s, i)
                t = wait_filled(dve, "cb", s, i)
                h = hid[:, n * i:n * (i + 1), P * (t0 % NT):P * (t0 % NT + nt)]
                tt(h, t[:, :].rearrange("p (a n) -> p a n", a=n), h, ALU.mult).then_inc(is_freed("cb", s, i), 1)

            def finish(s):
                t0, nt = SEG[s]
                t = wait_filled(dve, "zT", s)
                tv = t[:, 0:64 * nt].rearrange("p (i c m) -> p c i m", c=2, m=D)
                r = h2_sb[:, t0:t0 + nt, :].rearrange("p (c i) m -> p c i m", c=2)
                tt(r, tv, r, ALU.add).then_inc(is_freed("zT", s), 1)

            def blocks():
                pool_softmax(0)
                pool_sum(0, 0)
                pool_sum(0, 1)
                ln1(0, 1)
                pool_sum(0, 2)
                xs_lo(0)
                pool_sum(0, 3)
                ln1(1, 1)
                xs_lo(1)
                pool_softmax(1)
                pool_sum(1, 0)
                key_gains()
                keys(0)
                pool_sum(1, 1)
                pool_sum(1, 2)
                ssq_out(0)
                pool_sum(1, 3)
                query_scales(0)
                ln1(2, 2)
                attn(0, {2: [lambda: xs_lo(2)], 3: [lambda: xs_lo(3)]})
                keys(1)
                ln2(0)
                ssq_out(1)
                query_scales(1)
                xs2_lo(0)
                router(0)
                top2(0)
                attn(1, {**{i + 1: [lambda i=i: gate_hidden(0, i)] for i in range(4)}, 6: [lambda: finish(0)]})
                ln2(1)
                xs2_lo(1)
                router(1)
                top2(1)
                ln2(2)
                gate_hidden(1, 0)
                xs2_lo(2)
                gate_hidden(1, 1)
                router(2)
                top2(2)
                finish(1)
                for i in range(2):
                    gate_hidden(2, i)
                finish(2)

            blocks()

        @block.tensor
        def _(pe):
            mm, turn = nc.tensor.matmul, nc.tensor.transpose

            def claim(*key):
                r = region_of[key]
                if use_of[key] > 1:
                    pe.wait_ge(freed[r], use_of[key] - 1)
                return ps[r]

            def done(ins, *key):
                ins.then_inc(filled[region_of[key]], 1)

            def score(hf):
                pe.wait_ge(s_tokw, 48)
                o = claim("score", hf)
                for g in range(2):
                    pe.wait_ge(s_x[hf][g], 16)
                    for jj in range(8):
                        i = mm(o[64 * hf + 32 * g:64 * hf + 32 * g + 32, 0:TIME], wz[:, 30 - 2 * jj:62 - 2 * jj],
                               x_sb[:, NJ * hf + 8 * g + jj, :], start=jj == 0, stop=jj == 7)
                done(i, "score", hf)

            def wb(hf, q):
                pe.wait_ge(S["selectors"], 1)
                pe.wait_ge(S["pool_w_ready"], hf + 1)
                o = claim("wb", hf, q)
                for j in range(4):
                    jj = 4 * q + j
                    i = mm(o[:, TIME * j:TIME * (j + 1)], row_sel[:, 2 * jj:2 * jj + 2, :].rearrange("p a f -> p (a f)"),
                           pool_ws[:, hf, :], start=True, stop=True)
                done(i, "wb", hf, q)

            def hT(q):
                by_pool = sum(m % 4 in GPSIMD_SUMS[m // 4] for m in range(2 * q + 2))
                pe.wait_ge(S["pooled"], 2 * q + 2 - by_pool)
                if by_pool:
                    pe.wait_ge(S["pooled_p"], by_pool)
                o = claim("hT", q)
                for j in range(2):
                    c = P * (2 * (q % 2) + j)
                    i = turn(o[:, P * j:P * j + P], pooledT[:, c:c + P], ident)
                done(i, "hT", q)

            def xT(q):
                pe.wait_ge(S["ln_ready"], q + 1)
                o = claim("xT", q)
                for T in range(4):
                    i = turn(o[:, P * T:P * T + P], ln_sb[:, 4 * (q % 2) + T, :, :].rearrange("p c d -> p (c d)"), ident)
                done(i, "xT", q)

            def kv(q):
                wait_freed(pe, "xT", q)
                pe.wait_ge(S["weights_ready"], 2)
                o = claim("kv", q)
                for T in range(4):
                    x_ = xs[:, 512 * (q % 2) + P * T:512 * (q % 2) + P * T + P]
                    for part in range(2):
                        i = mm(o[:, P * T:P * T + P], x_, wkvT[:, part, :], start=part == 0, stop=part == 1)
                done(i, "kv", q)

            def A(hf, c, q):
                pe.wait_ge(S["weights_ready"], 1)
                wait_freed(pe, "xT", 2 * hf + c)
                o = claim("A", hf, c, q)
                for a in range(2):
                    p = 2 * q + a
                    for part in range(2):
                        i = mm(o[:, 512 * a:512 * a + 512], wqT[:, part, P * p:P * p + P], xs[:, 512 * c:512 * c + 512],
                               start=part == 0, stop=part == 1)
                done(i, "A", hf, c, q)

            def KT(hf):
                pe.wait_ge(S["kn_ready"], hf + 1)
                o = claim("KT", hf)
                for T in range(NT):
                    i = turn(o[:, P * T:P * T + P], kn[:, T, :, :].rearrange("p c d -> p (c d)"), ident)
                done(i, "KT", hf)

            def square_sums(hf, p):
                pe.wait_ge(S["q_squared_p"], NPAIR * hf + p + 1)
                pe.wait_ge(S["q_squared"], NPAIR * hf + p + 1)
                o = claim("ss", hf) if p == 0 else ps[region_of["ss", hf]]
                for c in range(4):
                    i = mm(o[32 * c:32 * c + 32, 0:256], cst[:, C_ONES + 32 * p:C_ONES + 32 * p + 32],
                           sq_sb[:, p % SQ_RING, 256 * c:256 * c + 256], start=p == 0, stop=p == NPAIR - 1)
                if p < NPAIR - 1:
                    i.then_inc(S["squares_used"], 1)
                else:
                    done(i, "ss", hf)

            def ssT(hf):
                wait_freed(pe, "ss", hf)
                o = claim("ssT", hf)
                for j in range(2):
                    i = turn(o[:, P * j:P * j + P], ssq_sb[:, P * j:P * j + P], ident)
                done(i, "ssT", hf)

            def Dj(hf, k):
                pe.wait_ge(s_rot, 16)
                if k == 0:
                    wait_freed(pe, "A", hf, 1, 2)
                    wait_freed(pe, "A", hf, 1, 3)
                o = claim("D", hf, k)
                qv = q_sb[:, :, :].rearrange("p a (b t) -> p a b t", t=W)
                for t in range(4):
                    i = mm(o[:, 256 * t:256 * t + 256], rot_sb[:, 4 * k + t, :], qv[:, :, :, 4 * k + t],
                           start=True, stop=True)
                done(i, "D", hf, k)

            def Sj(hf, T):
                if T == 0:
                    wait_freed(pe, "D", hf, 6)
                    wait_freed(pe, "D", hf, 7)
                    wait_freed(pe, "KT", hf)
                o = claim("S", hf, T)
                for g in range(2):
                    for j4 in range(4):
                        b = 4 * T + j4
                        i = mm(o[:, 512 * g + P * j4:512 * g + P * j4 + P],
                               qr_sb[:, b, 4 * g:4 * g + 4, :].rearrange("p a t -> p (a t)"),
                               key_block[:, b:b + 2, :].rearrange("p b s -> p (b s)"), start=True, stop=True)
                done(i, "S", hf, T)

            def PT(hf, T):
                n = NT * hf + T
                pe.wait_ge(S["prob_ready"], n + 1)
                o = claim("PT", hf, T)
                for g in range(2):
                    for r in range(2):
                        c = P * (2 * g + r)
                        i = turn(o[:, c:c + P], prob[:, n % PROB_RING, g, 2 * r:2 * r + 2, :, :].rearrange("p j h s -> p (j h s)"),
                                 ident)
                done(i, "PT", hf, T)

            def PV(hf, T):
                n = NT * hf + T
                wait_freed(pe, "PT", hf, T)
                pe.wait_ge(S["values_in"], 4 * (hf + 1))
                o = claim("PV", hf, T)
                for j4 in range(4):
                    i = mm(o[:, 256 * j4:256 * j4 + 256], value_block[:, 4 * T + j4, :],
                           probT[:, n % 2, j4 // 2, :, :].rearrange("p g n -> p (g n)"), start=True, stop=True)
                done(i, "PV", hf, T)

            def OP(q):
                wait_freed(pe, "PV", q // 2, 4 * (q % 2) + 3)
                pe.wait_ge(s_wo, 16)
                o = claim("OP", q)
                for a in range(NPAIR):
                    for c in range(2):
                        x0 = 512 * (q % 2) + 256 * c
                        i = mm(o[64 * c:64 * c + 64, 0:256], woT[:, a, :], o_sb[:, a, x0:x0 + 256],
                               start=a == 0, stop=a == NPAIR - 1)
                done(i, "OP", q)

            def turned(src, x0, n, src_key, *key):
                wait_freed(pe, *src_key)
                o = claim(*key)
                for j in range(n):
                    i = turn(o[:, P * j:P * j + P], src[:, x0 + P * j:x0 + P * j + P], ident)
                done(i, *key)

            def x2T(s):
                t0, nt = SEG[s]
                pe.wait_ge(S["ln2_ready"], s + 1)
                o = claim("x2T", s)
                for T in range(nt):
                    i = turn(o[:, P * T:P * T + P], ln2_sb[:, t0 % NT + T, :, :].rearrange("p c d -> p (c d)"), ident)
                done(i, "x2T", s)

            def lg(s):
                t0, nt = SEG[s]
                wait_freed(pe, "x2T", s)
                o = claim("lg", s)
                for T in range(nt):
                    c = P * (t0 % NT + T)
                    for part in range(2):
                        i = mm(o[:, E * T:E * T + E], xs2[:, c:c + P], routerT[:, part, :],
                               start=part == 0, stop=part == 1)
                done(i, "lg", s)

            def cT(s):
                t0, nt = SEG[s]
                pe.wait_ge(S["gate_ready"], s + 1)
                o = claim("cT", s)
                for T in range(nt):
                    i = turn(o[0:2 * E, P * T:P * T + P], gate[:, t0 + T, :].bitcast(F32), ident)
                done(i, "cT", s)

            def L1(s, i):
                t0, nt = SEG[s]
                wait_freed(pe, "x2T", s)
                pe.wait_ge(S["weights_ready"], 4)
                o = claim("L1", s, i)
                for c in range(2):
                    pr, x0 = (i, 512 * c) if nt == 8 else (2 * i + c, P * (t0 % NT))
                    for part in range(2):
                        ins = mm(o[:, 512 * c:512 * c + 512], w1s[:, part, P * pr:P * pr + P],
                                 xs2[:, x0:x0 + 512], start=part == 0, stop=part == 1)
                done(ins, "L1", s, i)

            def cb(s, i):
                t0, nt = SEG[s]
                pe.wait_ge(S["selectors"], 2)
                wait_freed(pe, "cT", s)
                o = claim("cb", s, i)
                for c in range(2):
                    pr, x0 = (i, 512 * c) if nt == 8 else (2 * i + c, P * (t0 % NT))
                    ins = mm(o[:, 512 * c:512 * c + 512], expert_sel[:, pr, :], gateT[:, x0:x0 + 512], start=True, stop=True)
                done(ins, "cb", s, i)

            def L2(s):
                t0, nt = SEG[s]
                pe.wait_ge(s_wff, 64)
                o = claim("L2", s)
                n = 64 * nt
                col = [P * (t0 % NT) + n * c for c in range(2)]
                for c in range(2):
                    mm(o[64 * c:64 * c + 64, 0:n], b2_sb[:, :], gateT[:, col[c]:col[c] + n].bitcast(F32),
                       start=True, stop=False)
                for pr in range(4):
                    wait_freed(pe, "cb", s, pr * nt // 8)
                    for c in range(2):
                        i = mm(o[64 * c:64 * c + 64, 0:n], w2_sb[:, pr, :], hid[:, pr, col[c]:col[c] + n],
                               start=False, stop=pr == 3)
                done(i, "L2", s)

            run = {"score": score, "wb": wb, "hT": hT, "xT": xT, "kv": kv, "A": A,
                   "KT": KT, "ss": lambda hf: None, "squares": square_sums, "ssT": ssT, "D": Dj, "S": Sj, "PT": PT, "PV": PV, "OP": OP,
                   "yT": lambda q: turned(y_sb, 256 * (q % 2), 2, ("OP", q), "yT", q), "x2T": x2T, "lg": lg, "cT": cT, "L1": L1,
                   "cb": cb, "L2": L2, "zT": lambda s: turned(z_sb, 256 * (s == 2), SEG[s][1] // 2, ("L2", s), "zT", s)}
            for key, _ in jobs:
                run[key[0]](*key[1:])


def kernel(**inputs):
    import concourse.bacc as bacc
    from concourse.bass_utils import run_bass_kernel_spmd

    nc = bacc.Bacc("TRN2", target_bir_lowering=False, num_devices=1)
    a = {name.removeprefix("L0_"): np.asarray(v) for name, v in inputs.items()}
    const, rot = shape_constants()
    arrays = {
        "x": a["x"], "tok_w_t": a["tok_w"].T, "tok_b": a["tok_b"], "wq_t": a["attn_wq"].T, "wkv_t": a["attn_wkv"].T,
        "wo_t": a["attn_wo"].reshape(D, NPAIR, P).transpose(2, 1, 0).reshape(P, NPAIR * D),
        "q_norm_w": a["attn_q_norm_w"], "k_norm_w": a["attn_k_norm_w"], "router_t": a["ffn_router_w"].T,
        "w1_t": a["ffn_w1"].transpose(1, 0, 2).reshape(D, E * D),
        "b1_t": a["ffn_b1"].reshape(E // 2, P).T, "w2": a["ffn_w2"], "b2": a["ffn_b2"], "const": const, "rot": rot}
    arrays = {name: np.ascontiguousarray(v) for name, v in arrays.items()}
    args = [nc.dram_tensor(name, v.shape, mybir.dt.from_np(v.dtype), kind="ExternalInput").ap()
            for name, v in arrays.items()]
    args.append(nc.dram_tensor("out", (B, W, F), F32, kind="ExternalOutput").ap())
    audio_tower(nc, *args)
    return run_bass_kernel_spmd(nc, [arrays], core_ids=[0]).results[0]["out"]
```

```python
from contextlib import ExitStack

import numpy as np

import concourse.bass as bass
from concourse import mybir

F32 = mybir.dt.float32
F32R = mybir.dt.float32r
I32 = mybir.dt.int32
ALU = mybir.AluOpType
ACT = mybir.ActivationFunctionType
AX = mybir.AxisListType.X

B, F, TIME, K = 64, 64, 256, 8
W = TIME // K
D = F
H = 16
E = 8
P = 128
NPAIR = H // 2
HALVES = 2
RB = B // HALVES
NT = RB * W // P
TOK = NT * P
NJ = B // 2 // HALVES
EPS_LN = 1e-5
EPS_RMS = 1.1920929e-07
NEG = -1e30
RSQRT_MAGIC = 0x5F3759DF
SEG = [(0, NT), (NT, NT // 2), (NT + NT // 2, NT // 2)]
GPSIMD_SUMS = [(2,), (1, 2, 3)]
SQ_RING = 4
PROB_RING = 4
FILLERS = {("score", 0): 6, ("wb", 0, 0): 8, ("hT", 0): 10, ("xT", 0): 11, ("wb", 0, 3): 1, ("A", 0, 0, 0): 1,
           ("hT", 1): 1, ("xT", 1): 3, ("A", 0, 1, 0): 1, ("PT", 0, 0): 3, ("x2T", 2): 1}

C_ID, C_COS, C_SIN, C_MASK, C_SELC, C_ONES, C_IDX, C_ROW, C_END = np.cumsum(
    [0, P, D, D, W, (E // 2) * P, NPAIR * 32, E, 32]).tolist()


def shape_constants():
    c = np.zeros((P, C_END), np.float32)
    p = np.arange(P)
    c[:, C_ID:C_COS] = np.eye(P)
    freqs = np.float32(10000.0) ** (np.float32(-2.0) * np.arange(D // 2, dtype=np.float32) / np.float32(D))
    theta = np.arange(W, dtype=np.float32)[:, None] * freqs[None, :].astype(np.float32)
    cos, sin = np.cos(theta).astype(np.float32), np.sin(theta).astype(np.float32)
    c[:, C_COS:C_SIN] = np.repeat(cos, 2, axis=1)[p % W]
    c[:, C_SIN:C_MASK] = (np.repeat(sin, 2, axis=1) * np.tile([-1.0, 1.0], D // 2))[p % W]
    c[:, C_MASK:C_SELC] = np.where(np.arange(W)[None, :] <= (p % W)[:, None], 0.0, NEG)
    q = np.arange(32)
    c[:, C_ROW:C_END] = (p[:, None] % 64) == (32 * (q // 16) + q % 16)[None, :]
    for pr in range(E // 2):
        for e2 in range(2):
            rows = [r for r in range(2 * E) if r % E == 2 * pr + e2]
            c[rows, C_SELC + pr * P + 64 * e2:C_SELC + pr * P + 64 * e2 + 64] = 1.0
    for pair in range(NPAIR):
        for h2 in range(2):
            c[64 * h2:64 * h2 + 64, C_ONES + pair * 32 + 2 * pair + h2] = 1.0
    c[:, C_IDX:C_ROW] = (E - np.arange(E))[None, :]
    rot = np.zeros((P, W, P), np.float32)
    for h2 in range(2):
        for i in range(D // 2):
            a, b = 64 * h2 + 2 * i, 64 * h2 + 2 * i + 1
            rot[a, :, a], rot[b, :, b] = cos[:, i], cos[:, i]
            rot[b, :, a], rot[a, :, b] = -sin[:, i], sin[:, i]
    return c, rot.reshape(P, W * P)


def pe_order():
    jobs = []

    def add(region, *key):
        jobs.append((key, region))

    turn = [0]

    def add01(*key):
        add("P%d" % (turn[0] % 2), *key)
        turn[0] += 1

    def squares(hf, pairs):
        for p in pairs:
            add("", "squares", hf, p)

    def attention(hf, extra, between={}):
        for T in range(NT + 4):
            if T < NT:
                add01("S", hf, T)
            if 3 <= T < NT + 3:
                add("B4", "PT", hf, T - 3)
            for f in between.get(T, []):
                f()
            if T > NT:
                add01("PV", hf, T - 4)
            elif T >= 4:
                add("P2", "PV", hf, T - 4)
            for f in extra.get(T, []):
                f()

    def one(region, *key):
        return lambda: add(region, *key)

    add("B5", "score", 0)
    add("P2", "wb", 0, 0)
    add("P0", "wb", 0, 1)
    add("B4", "hT", 0)
    add("P2", "wb", 0, 2)
    add("B5", "xT", 0)
    add("P2", "wb", 0, 3)
    turn[0] = 1
    add01("A", 0, 0, 0)
    add("B4", "hT", 1)
    add("B5", "score", 1)
    add01("A", 0, 0, 1)
    add01("A", 0, 0, 2)
    add01("A", 0, 0, 3)
    add("B4", "xT", 1)
    add("P2", "kv", 0)
    add01("A", 0, 1, 0)
    add("P2", "kv", 1)
    add01("A", 0, 1, 1)
    add01("A", 0, 1, 2)
    add01("A", 0, 1, 3)
    add("P2", "wb", 1, 0)
    for k in range(8):
        add01("D", 0, k)
        if k == 0:
            add("B5", "ss", 0)
        if k == 1:
            squares(0, range(4))
            add("P2", "wb", 1, 1)
        if k == 2:
            add("P2", "wb", 1, 2)
        if k == 3:
            squares(0, range(4, 8))
            add("P2", "wb", 1, 3)
        if k == 4:
            add("B4", "ssT", 0)
        if k == 5:
            add("B5", "hT", 2)
            add("P2", "KT", 0)
        if k == 6:
            add("B4", "hT", 3)
    attention(0, {1: [one("B5", "xT", 2)], 3: [one("B5", "xT", 3)], 5: [one("B5", "kv", 2)], 6: [one("B5", "kv", 3)],
                  8: [one("B5", "OP", 0)], 9: [lambda: add01("A", 1, 0, 0), lambda: add01("A", 1, 0, 1)],
                  10: [lambda: add01("A", 1, 0, 2)], 11: [lambda: add01("A", 1, 0, 3), one("B4", "yT", 0)]})
    add("B5", "OP", 1)
    for q in range(4):
        add01("A", 1, 1, q)
        if q == 0:
            add("B4", "yT", 1)
    add("P2", "KT", 1)
    for k in range(8):
        add01("D", 1, k)
        if k == 0:
            add("B5", "ss", 1)
        if k == 1:
            squares(1, range(4))
        if k == 2:
            add("P2", "x2T", 0)
        if k == 3:
            squares(1, range(4, 8))
            add("B4", "lg", 0)
        if k == 4:
            add("B4", "ssT", 1)
    add01("L1", 0, 0)
    add01("L1", 0, 1)
    add("P2", "L1", 0, 2)
    attention(1, {0: [one("P2", "L1", 0, 3)], 1: [one("P2", "cT", 0), one("P2", "cb", 0, 0)],
                  2: [one("P2", "cb", 0, 1)], 3: [one("P2", "cb", 0, 2)], 4: [one("P2", "cb", 0, 3)],
                  7: [one("B5", "OP", 2)], 10: [one("B5", "x2T", 1)], 11: [one("B5", "lg", 1)]},
              {8: [one("B4", "yT", 2)]})
    add("B5", "OP", 3)
    add("B4", "yT", 3)
    add("P2", "cT", 1)
    for i in range(2):
        add01("L1", 1, i)
    add("P2", "cb", 1, 0)
    add("B5", "L2", 0)
    add("B4", "x2T", 2)
    add01("cb", 1, 1)
    add("B4", "lg", 2)
    add("", "L2_end", 0)
    add("B4", "zT", 0)
    for i in range(2):
        add01("L1", 2, i)
    add("B5", "L2", 1)
    add("P2", "cT", 2)
    add("", "L2_end", 1)
    add("P2", "cb", 2, 0)
    add01("cb", 2, 1)
    add("B4", "zT", 1)
    add("B5", "L2", 2)
    add("", "L2_end", 2)
    add("B4", "zT", 2)
    return jobs


def audio_tower(nc, x, tok_w_t, tok_b, wq_t, wkv_t, wo_t, q_norm_w, k_norm_w, router_t, w1_t, b1_t, w2, b2,
                const, rot, out):
    jobs = pe_order()
    region_of, use_of, uses = {}, {}, {}
    for key, region in jobs:
        uses[region] = uses.get(region, 0) + 1
        region_of[key], use_of[key] = region, uses[region]

    with ExitStack() as ctx:
        def sb(name, shape, dt=F32):
            return ctx.enter_context(nc.sbuf_tensor(name, shape, dt))

        def sem(name):
            return ctx.enter_context(nc.semaphore(name))

        ps = {r: ctx.enter_context(nc.psum_tensor("ps_" + r, [P, 1024], F32)) for r in ("P0", "P1", "P2")}
        ps |= {r: ctx.enter_context(nc.psum_tensor("ps_" + r, [P, 512], F32)) for r in ("B4", "B5")}
        filled = {r: sem("filled_" + r) for r in ps}
        freed = {r: sem("freed_" + r) for r in ps}

        qr_sb = sb("qr_sb", [P, RB, NPAIR, W])
        raw = qr_sb[:, :, :, :].rearrange("p b a t -> p (b a t)")
        wq_raw, wkv_raw, w1_raw, router_raw = (raw[:, a:b] for a, b in ((0, 1024), (1024, 1152), (1152, 1664), (1664, 1672)))
        cst = sb("cst", [P, C_END])
        ident = cst[:, C_ID:C_COS]
        rot_sb = sb("rot_sb", [P, W, P])
        w2_sb = sb("w2_sb", [P, E // 2, D])
        b1_sb = sb("b1_sb", [P, E // 2])
        b2_sb = sb("b2_sb", [P, D])
        norm_w = sb("norm_w", [P, 2, D])
        key_gain = sb("key_gain", [P, D])
        tokb_sb = sb("tokb_sb", [P, 1])
        wz = sb("wz", [P, 64])
        zeros = sb("zeros", [P, 256])
        first_exp = sb("first_exp", [P, 1])
        wqT = sb("wqT", [P, 2, H * D], F32R)
        wkvT = sb("wkvT", [P, 2, P], F32R)
        routerT = sb("routerT", [P, 2, E], F32R)
        w1s = sb("w1s", [P, 2, E * D], F32R)
        woT = sb("woT", [P, NPAIR, D])
        row_sel = sb("row_sel", [P, 32, D], F32R)
        expert_sel = sb("expert_sel", [P, E // 2, P], F32R)

        x_sb = sb("x_sb", [P, HALVES * NJ, TIME])
        score_sb = sb("score_sb", [P, TIME])
        pool_w = sb("pool_w", [P, TIME])
        pool_ws = sb("pool_ws", [P, HALVES, TIME], F32R)
        win_stat = sb("win_stat", [P, 3, W])
        prod = sb("prod", [P, 2, 4 * TIME])
        pooledT = sb("pooledT", [P, NJ * W])
        after_x = x_sb[:, :, :].rearrange("p j t -> p (j t)")
        KEYS = (RB + 1) * 2 * W
        value_block = after_x[:, KEYS:KEYS + RB * P].rearrange("p (b m) -> p b m", b=RB)
        key_block = after_x[:, 0:KEYS].rearrange("p (b s) -> p b s", b=RB + 1)
        Y = KEYS + RB * P
        y_sb = after_x[:, Y:Y + 512]
        rq_stat = after_x[:, Y + 512:Y + 896].rearrange("p (a n) -> p a n", a=3)
        z_sb = after_x[:, Y + 896:Y + 1408]
        after_prod = prod[:, :, :].rearrange("p r n -> p (r n)")
        probT = after_prod[:, 0:1024].rearrange("p (r q g n) -> p r q g n", r=2, q=2, g=2)
        h2_sb = after_prod[:, 1024:2048].rearrange("p (n f) -> p n f", f=D)
        gateT = row_sel[:, :, :].rearrange("p a f -> p (a f)")
        h_sb = sb("h_sb", [P, HALVES * NT, D])
        ktmp = sb("ktmp", [P, 2, NT, D])
        key_tmp = sb("key_tmp", [P, NT, D])
        ln_sb = sb("ln_sb", [P, NT, 2, D])
        stat = sb("stat", [P, 8, NT])
        xs = sb("xs", [P, TOK], F32R)
        kv_sb = sb("kv_sb", [P, NT, P])
        kn = sb("kn", [P, NT, 2, D])
        q_sb = sb("q_sb", [P, NPAIR, TOK])
        o_sb = q_sb
        sq_sb = sb("sq_sb", [P, SQ_RING, TOK])
        ssq_sb = sb("ssq_sb", [P, 256])
        prob = sq_sb[:, 0:2, :].rearrange("p q n -> p (q n)").rearrange("p (r g j h s) -> p r g j h s", r=PROB_RING, g=2, j=4, h=2)
        rq = sb("rq", [P, HALVES, NT, 2, 4, 2])
        row_stat = sb("row_stat", [P, PROB_RING, 3, 16])
        ln2_sb = ln_sb
        xs2 = xs
        rt = sb("rt", [P, 8, NT, E])
        r1 = sb("r1", [P, 6, NT])
        gate = sb("gate", [P, HALVES * NT, 2 * E], F32R)
        hid = rot_sb[:, :, :].rearrange("p t m -> p (t m)").rearrange("p (r n) -> p r n", r=E // 2)

        s_row, s_cst, s_rot, s_tokw, s_tokb, s_wq, s_wsm, s_w1, s_wff, s_wo, s_out = (
            sem(n) for n in ("row_in", "cst_in", "rot_in", "tokw_in", "tokb_in", "wq_in", "wsmall_in", "w1_in", "wffn_in", "wo_in", "out_stored"))
        s_x = [[sem(f"x_in{h}{g}") for g in range(2)] for h in range(HALVES)]
        names = ("wz_zero zeros_ready zeroed weights_hi weights_ready row_selectors expert_selectors dve_link score_shift pool_exp pool_w_ready pooled pooled_p "
                 "ln_ready xs_hi kn_ready values_in q_squared q_squared_p squares_used keys_rotated pool_link scales scales_moved masked logits_ready prob_exp "
                 "prob_sums prob_ready ln2_ready xs2_hi gate_exp gate_ready").split()
        S = {n: sem(n) for n in names}
        block = ctx.enter_context(nc.Block())

        def wait_filled(eng, *key):
            r = region_of[key]
            eng.wait_ge(filled[r], use_of[key])
            return ps[r]

        def is_freed(*key):
            return freed[region_of[key]]

        def wait_freed(eng, *key):
            eng.wait_ge(freed[region_of[key]], use_of[key])

        def gate_cols(s):
            return P * SEG[s][0]

        def hidden(s):
            t0, nt = SEG[s]
            if s == 1:
                return sq_sb[:, 2:4, :].rearrange("p q n -> p (q n)").rearrange("p (r n) -> p r n", r=E // 2)
            return hid[:, :, P * (t0 % NT):P * (t0 % NT + nt)]

        def move_scales(copy, hf):
            yv = rq_stat[:, 1, :].rearrange("p (n g a h) -> p n g a h", n=NT, g=2, a=4)
            for j4 in range(4):
                for a in range(4):
                    last = copy(rq[32 * a:32 * a + 32, hf, :, :, j4, :], yv[32 * j4:32 * j4 + 32, :, :, a, :])
            return last

        def rotated(k):
            return qr_sb[:, :, :, 4 * k:4 * k + 4].rearrange("p b a t -> p t a b")

        def square_slot_free(eng, hf, p):
            if p >= SQ_RING:
                eng.wait_ge(S["squares_used"], (NPAIR - 1) * hf + p - SQ_RING + 1)
            elif hf:
                wait_filled(eng, "PT", 0, NT - 1)

        @block.sync
        def _(sp):
            xv = x.rearrange("(j c) f t -> (c f) j t", c=2)
            for hf in range(HALVES):
                if hf:
                    sp.wait_ge(s_x[0][0], 16)
                for g in range(2):
                    j = NJ * hf + 8 * g
                    sp.dma_start(x_sb[:, j:j + 8, :], xv[:, j:j + 8, :]).then_inc(s_x[hf][g], 16)
                    if j == 0:
                        sp.wait_ge(S["wz_zero"], 1)
                        sp.dma_start(wz[64:128, 31:32], tok_w_t).then_inc(s_tokw, 16)
            for c in range(2):
                sp.dma_start(router_raw[D * c:D * c + D, :], router_t).then_inc(s_wsm, 16)
            sp.dma_start(norm_w[:, 0, :], q_norm_w.rearrange("(a d) -> a d", a=1).to_broadcast([P, D])).then_inc(s_wsm, 16)
            sp.dma_start(norm_w[:, 1, :], k_norm_w.rearrange("(a d) -> a d", a=1).to_broadcast([P, D])).then_inc(s_wsm, 16)
            sp.dma_start(w1_raw[0:64, :], w1_t).then_inc(s_w1, 16)
            sp.dma_start(w1_raw[64:128, :], w1_t).then_inc(s_w1, 16)
            sp.dma_start(rot_sb[:, :, :], rot.rearrange("p (t m) -> p t m", t=W)).then_inc(s_rot, 16)
            sp.dma_start(w2_sb[:, :, :], w2.rearrange("(a e) f m -> (e f) a m", e=2)).then_inc(s_wff, 16)
            sp.dma_start(b1_sb[:, :], b1_t).then_inc(s_wff, 16)
            sp.dma_start(woT[:, :, :], wo_t.rearrange("p (a m) -> p a m", a=NPAIR)).then_inc(s_wo, 16)
            sp.wait_ge(S["zeroed"], 1)
            sp.dma_start(b2_sb[0:E, :], b2).then_inc(s_wff, 16)
            sp.dma_start(b2_sb[E:2 * E, :], b2).then_inc(s_wff, 16)
            for s, (t0, nt) in enumerate(SEG):
                wait_freed(sp, "zT", s)
                sp.dma_start(out[:, t0:t0 + nt, :], h2_sb[:, t0:t0 + nt, :]).then_inc(s_out, 16)
            sp.wait_ge(s_out, 16 * len(SEG))

        @block.gpsimd
        def _(pool):
            def rows(n):
                return prob[:, n % PROB_RING, :, :, :, :].rearrange("p g j h s -> p (g j h) s")

            def scale(hf, T):
                n = NT * hf + T
                pool.wait_ge(S["masked"], n + 1)
                link(nc.gpsimd.tensor_tensor(rows(n), rows(n), row_stat[:, n % PROB_RING, 0, :].unsqueeze(2).to_broadcast([P, 16, W]),
                                             ALU.subtract))
                pool.wait_ge(S["scales_moved"], hf + 1)
                r = rq[:, hf, T, :, :, :].rearrange("p g j h -> p (g j h)")
                nc.gpsimd.tensor_tensor(rows(n), rows(n), r.unsqueeze(2).to_broadcast([P, 16, W]),
                                        ALU.mult).then_inc(S["logits_ready"], 1)

            def normalise(hf, T):
                n = NT * hf + T
                pool.wait_ge(S["prob_sums"], n + 1)
                nc.gpsimd.tensor_tensor(rows(n), rows(n), row_stat[:, n % PROB_RING, 2, :].unsqueeze(2).to_broadcast([P, 16, W]),
                                        ALU.mult).then_inc(S["prob_ready"], 1)

            nc.gpsimd.memset(wz[:, :], 0.0).then_inc(S["wz_zero"], 1)
            nc.gpsimd.memset(zeros[:, :], 0.0).then_inc(S["zeros_ready"], 1)
            nc.gpsimd.memset(b2_sb[:, :], 0.0).then_inc(S["zeroed"], 1)

            def squares(hf, p):
                wait_freed(pool, "A", hf, 0, p // 2)
                square_slot_free(pool, hf, p)
                nc.gpsimd.tensor_tensor(sq_sb[:, p % SQ_RING, 0:512], q_sb[:, p, 0:512], q_sb[:, p, 0:512],
                                        ALU.mult).then_inc(S["q_squared_p"], 1)

            steps = [0]

            def link(ins):
                steps[0] += 1
                ins.then_inc(S["pool_link"], 1)
                pool.wait_ge(S["pool_link"], steps[0])

            def rope(hf):
                wait_freed(pool, "kv", 2 * hf)
                wait_freed(pool, "kv", 2 * hf + 1)
                mul = nc.gpsimd.tensor_tensor
                k, b = kv_sb[:, :, 0:D], key_tmp[:, :, :]
                cos, sin = (cst[:, o:o + D].unsqueeze(1).to_broadcast([P, NT, D]) for o in (C_COS, C_SIN))
                kp, bp, sp_ = (a.rearrange("p n (i c) -> p n i c", c=2) for a in (k, b, sin))
                for c in range(2):
                    link(mul(bp[:, :, :, c], kp[:, :, :, 1 - c], sp_[:, :, :, c], ALU.mult))
                link(mul(k, k, cos, ALU.mult))
                link(mul(k, k, b, ALU.add))
                mul(b, k, k, ALU.mult).then_inc(S["keys_rotated"], 1)

            def lo_part(parts, raw_w):
                nc.gpsimd.tensor_tensor(parts[:, 1, :], raw_w, parts[:, 0, :].bitcast(F32), ALU.subtract)\
                    .then_inc(S["weights_ready"], 1)

            def window_sum(hf, i):
                n = 4 * hf + i
                wait_freed(pool, "wb", hf, i)
                v = prod[:, n % 2, :].rearrange("p (w k) -> p w k", k=K)
                add_ = nc.gpsimd.tensor_tensor
                link(add_(v[:, :, 0:4], v[:, :, 0:4], v[:, :, 4:8], ALU.add))
                link(add_(v[:, :, 0:2], v[:, :, 0:2], v[:, :, 2:4], ALU.add))
                if hf:
                    wait_filled(pool, "hT", 1)
                add_(pooledT[:, 4 * W * i:4 * W * (i + 1)].unsqueeze(2), v[:, :, 0:1], v[:, :, 1:2], ALU.add)\
                    .then_inc(S["pooled_p"], 1)

            pool.wait_ge(S["weights_hi"], 1)
            lo_part(wqT, wq_raw)
            window_sum(0, 2)
            pool.wait_ge(S["weights_hi"], 3)
            lo_part(wkvT, wkv_raw)
            lo_part(routerT, router_raw)
            pool.wait_ge(s_w1, 32)
            link(nc.gpsimd.tensor_copy(w1s[:, 0, :], w1_raw))
            lo_part(w1s, w1_raw)
            pool.wait_ge(s_cst, 16)
            for p in range(4):
                squares(0, p)
            wait_freed(pool, "wb", 0, 3)
            nc.gpsimd.memset(key_block[:, :, :], 0.0).then_inc(S["zeroed"], 1)
            rope(0)
            for p in range(4, NPAIR):
                squares(0, p)
            for i in range(1, 4):
                window_sum(1, i)
            nc.gpsimd.memset(value_block[:, :, :], 0.0).then_inc(S["zeroed"], 1)
            for hf in range(HALVES):
                if hf:
                    for p in range(NPAIR):
                        squares(hf, p)
                for T in range(NT + 1):
                    if T < NT:
                        scale(hf, T)
                    if T >= 1:
                        normalise(hf, T - 1)
                if hf == 0:
                    rope(1)
                    wait_filled(pool, "wb", 1, 3)
                    nc.gpsimd.memset(gateT[:, :].bitcast(F32), 0.0).then_inc(S["zeroed"], 1)

        @block.scalar
        def _(act):
            act.dma_start(cst[:, C_ROW:C_END], const[:, C_ROW:C_END]).then_inc(s_row, 16)
            act.wait_ge(S["wz_zero"], 1)
            act.dma_start(wz[0:64, 30:31], tok_w_t).then_inc(s_tokw, 16)
            act.dma_start(tokb_sb[:, :], tok_b.rearrange("(a o) -> a o", a=1).to_broadcast([P, 1])).then_inc(s_tokb, 16)
            act.dma_start(cst[:, 0:C_ROW], const[:, 0:C_ROW]).then_inc(s_cst, 16)
            act.wait_ge(S["zeros_ready"], 1)
            nc.scalar.activation(first_exp[:, :], zeros[:, 0:1], ACT.Exp)
            for c in range(2):
                r = slice(D * c, D * c + D)
                act.dma_start(wq_raw[r, :], wq_t).then_inc(s_wq, 16)
                act.dma_start(wkv_raw[r, :], wkv_t).then_inc(s_wsm, 16)

            def copy(o, i):
                return nc.scalar.activation(o, i, ACT.Copy)

            def pool_exp(hf):
                r = slice(64 * hf, 64 * hf + 64)
                act.wait_ge(S["score_shift"], hf + 1)
                nc.scalar.activation(pool_w[r, :], score_sb[r, :], ACT.Exp).then_inc(S["pool_exp"], 1)

            def h_out(q):
                t = wait_filled(act, "hT", q)
                copy(h_sb[:, 4 * q:4 * q + 4, :], t[:, 0:256].rearrange("p (n f) -> p n f", f=D)).then_inc(is_freed("hT", q), 1)

            def xs_hi(q):
                t = wait_filled(act, "xT", q)
                if q >= 2:
                    wait_filled(act, "A", 0, 1, 3)
                    wait_filled(act, "kv", 1)
                copy(xs[:, 512 * (q % 2):512 * (q % 2) + 512], t[:, :]).then_inc(S["xs_hi"], 1)

            def kv_out(q):
                t = wait_filled(act, "kv", q)
                if q == 2:
                    act.wait_ge(S["values_in"], 4)
                copy(kv_sb[:, 4 * (q % 2):4 * (q % 2) + 4, :], t[:, 0:512].rearrange("p (n f) -> p n f", f=P))\
                    .then_inc(is_freed("kv", q), 1)

            def keys_in(hf):
                t = wait_filled(act, "KT", hf)
                act.wait_ge(S["zeroed"], 2)
                if hf:
                    wait_filled(act, "S", 0, NT - 1)
                for h2 in range(2):
                    r = slice(64 * h2, 64 * h2 + 64)
                    i = copy(key_block[r, 0:RB, W * h2:W * h2 + W], t[r, :].rearrange("p (b s) -> p b s", s=W))
                i.then_inc(is_freed("KT", hf), 1)

            def q_out(hf, c, q):
                t = wait_filled(act, "A", hf, c, q)
                if hf and q == 0:
                    wait_filled(act, "OP", c)
                copy(q_sb[:, 2 * q:2 * q + 2, 512 * c:512 * c + 512], t[:, :].rearrange("p (a n) -> p a n", a=2))\
                    .then_inc(is_freed("A", hf, c, q), 1)

            def q_square(hf, p):
                wait_freed(act, "A", hf, 1, p // 2)
                square_slot_free(act, hf, p)
                nc.scalar.activation(sq_sb[:, p % SQ_RING, 512:1024], q_sb[:, p, 512:1024],
                                     ACT.Square).then_inc(S["q_squared"], 1)

            def qr_out(hf, k):
                t = wait_filled(act, "D", hf, k)
                if k == 0 and hf:
                    wait_filled(act, "S", 0, NT - 1)
                elif k == 0:
                    act.wait_ge(S["weights_ready"], 4)
                copy(rotated(k), t[:, :].rearrange("p (t a b) -> p t a b", t=4, a=NPAIR)).then_inc(is_freed("D", hf, k), 1)

            def values_in(hf, j4):
                wait_freed(act, "kv", 2 * hf)
                wait_freed(act, "kv", 2 * hf + 1)
                if hf:
                    wait_filled(act, "PV", 0, NT - 1)
                else:
                    act.wait_ge(S["zeroed"], 3)
                vb = value_block[:, :, :].rearrange("p (n j) m -> p n j m", j=4)
                for h2 in range(2):
                    q = 2 * (j4 % 2) + h2
                    i = copy(vb[32 * q:32 * q + 32, :, j4, D * h2:D * h2 + D], kv_sb[32 * j4:32 * j4 + 32, :, D:2 * D])
                i.then_inc(S["values_in"], 1)

            def exp_out(hf, T):
                n = NT * hf + T
                act.wait_ge(S["logits_ready"], n + 1)
                e = prob[:, n % PROB_RING, :, :, :, :].rearrange("p g j h s -> p (g j h s)")
                nc.scalar.activation(e, e, ACT.Exp).then_inc(S["prob_exp"], 1)

            def attended_out(hf, T):
                t = wait_filled(act, "PV", hf, T)
                if T == 0:
                    wait_filled(act, "D", hf, 7)
                copy(o_sb[:, :, P * T:P * T + P].rearrange("p a (j t) -> p j a t", j=4),
                     t[:, :].rearrange("p (j a t) -> p j a t", j=4, a=NPAIR)).then_inc(is_freed("PV", hf, T), 1)

            def probT_out(hf, T):
                t = wait_filled(act, "PT", hf, T)
                copy(probT[:, T % 2, :, :, :], t[:, :].rearrange("p (g r n) -> p r g n", g=2, r=2))\
                    .then_inc(is_freed("PT", hf, T), 1)

            def attn(hf, extra):
                for T in range(NT + 4):
                    if 3 <= T < NT + 3:
                        probT_out(hf, T - 3)
                    if T >= 4:
                        attended_out(hf, T - 4)
                    if T < NT:
                        exp_out(hf, T)
                    for f in extra.get(T, []):
                        f()

            def y_out(q):
                t = wait_filled(act, "OP", q)
                o = 256 * (q % 2)
                copy(y_sb[:, o:o + 256], t[:, 0:256]).then_inc(is_freed("OP", q), 1)

            def xs2_hi(s):
                t0, nt = SEG[s]
                t = wait_filled(act, "x2T", s)
                if s == 0:
                    wait_filled(act, "A", 1, 1, 3)
                    wait_filled(act, "kv", 3)
                elif s == 1:
                    wait_filled(act, "L1", 0, 3)
                    wait_filled(act, "lg", 0)
                copy(xs2[:, P * (t0 % NT):P * (t0 % NT + nt)], t[:, 0:P * nt]).then_inc(S["xs2_hi"], 1)

            def gate_exp(s):
                nt = SEG[s][1]
                wait_freed(act, "lg", s)
                nc.scalar.activation(rt[:, 0, 0:nt, :], rt[:, 0, 0:nt, :], ACT.Exp).then_inc(S["gate_exp"], 1)

            def gateT_out(s):
                t0, nt = SEG[s]
                t = wait_filled(act, "cT", s)
                act.wait_ge(S["zeroed"], 4)
                copy(gateT[0:2 * E, gate_cols(s):gate_cols(s) + P * nt], t[0:2 * E, 0:P * nt]).then_inc(is_freed("cT", s), 1)

            def gelu(s):
                t0, nt = SEG[s]
                if s == 0:
                    act.wait_ge(s_wff, 64)
                if s != 1:
                    wait_filled(act, *(("L2", 0) if s else ("D", 1, 7)))
                for i in range(nt // 2):
                    t = wait_filled(act, "L1", s, i)
                    n = 8 // nt
                    for a in range(n):
                        pr = n * i + a
                        ins = nc.scalar.activation(hidden(s)[:, pr, :],
                                                   t[:, P * nt * a:P * nt * (a + 1)], ACT.Gelu, bias=b1_sb[:, pr:pr + 1])
                    ins.then_inc(is_freed("L1", s, i), 1)

            def z_out(s):
                n = 64 * SEG[s][1]
                o = 256 * (s == 2)
                t = wait_filled(act, "L2", s)
                if s:
                    wait_filled(act, "zT", 0)
                copy(z_sb[:, o:o + n], t[:, 0:n]).then_inc(is_freed("L2", s), 1)

            def rotated_out(hf):
                for p in range(4):
                    q_square(hf, p)
                qr_out(hf, 0)
                if hf:
                    keys_in(hf)
                    qr_out(hf, 1)
                for p in range(4, NPAIR):
                    q_square(hf, p)
                if hf == 0:
                    qr_out(hf, 1)
                qr_out(hf, 2)

            pool_exp(0)
            act.wait_ge(s_wq, 32)
            copy(wqT[:, 0, :], wq_raw).then_inc(S["weights_hi"], 1)
            h_out(0)
            xs_hi(0)
            act.wait_ge(s_wsm, 16 * 6)
            copy(wkvT[:, 0, :], wkv_raw).then_inc(S["weights_hi"], 1)
            copy(routerT[:, 0, :], router_raw).then_inc(S["weights_hi"], 1)
            q_out(0, 0, 0)
            h_out(1)
            for q in range(1, 4):
                q_out(0, 0, q)
            xs_hi(1)
            kv_out(0)
            q_out(0, 1, 0)
            kv_out(1)
            pool_exp(1)
            for q in range(1, 4):
                q_out(0, 1, q)
            rotated_out(0)
            for k in range(3, 6):
                qr_out(0, k)
            h_out(2)
            keys_in(0)
            qr_out(0, 6)
            h_out(3)
            qr_out(0, 7)
            act.wait_ge(S["scales"], 1)
            move_scales(copy, 0).then_inc(S["scales_moved"], 1)
            for j4 in range(4):
                values_in(0, j4)
            attn(0, {1: [lambda: xs_hi(2)], 3: [lambda: xs_hi(3)],
                     5: [lambda: kv_out(2)], 6: [lambda: kv_out(3)], 8: [lambda: y_out(0)],
                     9: [lambda: q_out(1, 0, 0), lambda: q_out(1, 0, 1)], 10: [lambda: q_out(1, 0, 2)],
                     11: [lambda: q_out(1, 0, 3)]})
            for j4 in range(3):
                values_in(1, j4)
            y_out(1)
            for q in range(4):
                q_out(1, 1, q)
            rotated_out(1)
            xs2_hi(0)
            qr_out(1, 3)
            qr_out(1, 4)
            gate_exp(0)
            qr_out(1, 5)
            qr_out(1, 6)
            qr_out(1, 7)
            gelu(0)
            attn(1, {0: [lambda: gateT_out(0)], 1: [lambda: values_in(1, 3)],
                     7: [lambda: y_out(2)], 10: [lambda: xs2_hi(1)], 11: [lambda: gate_exp(1)]})
            y_out(3)
            gateT_out(1)
            gelu(1)
            xs2_hi(2)
            gate_exp(2)
            z_out(0)
            gelu(2)
            gateT_out(2)
            z_out(1)
            z_out(2)

        @block.vector
        def _(dve):
            chain = [0]

            def link(ins):
                chain[0] += 1
                ins.then_inc(S["dve_link"], 1)
                dve.wait_ge(S["dve_link"], chain[0])

            tt, ts, red, stt = (nc.vector.tensor_tensor, nc.vector.tensor_scalar, nc.vector.tensor_reduce,
                                nc.vector.scalar_tensor_tensor)

            def bc(a, n):
                return a.unsqueeze(len(a.shape)).to_broadcast([*a.shape, n])

            def rsqrt(y, v, t):
                link(ts(t.bitcast(I32), v.bitcast(I32), 1, None, ALU.logical_shift_right))
                link(ts(y.bitcast(I32), t.bitcast(I32), -1.0, float(RSQRT_MAGIC), ALU.mult, ALU.add))
                for step in range(3):
                    link(tt(t, y, y, ALU.mult))
                    link(stt(out=t, in0=t, scalar=-0.5, in1=v, op0=ALU.mult, op1=ALU.mult))
                    last = stt(out=y, in0=t, scalar=1.5, in1=y, op0=ALU.add, op1=ALU.mult)
                    if step < 2:
                        link(last)
                return last

            dve.wait_ge(s_row, 16)
            nc.vector.tensor_copy(row_sel[:, :, :], bc(cst[:, C_ROW:C_END], D)).then_inc(S["row_selectors"], 1)

            def expert_selectors():
                dve.wait_ge(s_cst, 16)
                nc.vector.tensor_copy(expert_sel[:, :, :], cst[:, C_SELC:C_ONES].rearrange("p (a n) -> p a n", n=P))\
                    .then_inc(S["expert_selectors"], 1)

            def key_gains():
                dve.wait_ge(s_wsm, 16 * 6)
                link(stt(out=key_gain[:, :], in0=norm_w[:, 0, :], scalar=float(D) ** -0.5, in1=norm_w[:, 1, :],
                         op0=ALU.mult, op1=ALU.mult))

            def pool_softmax(hf):
                r = slice(64 * hf, 64 * hf + 64)
                t = wait_filled(dve, "score", hf)
                sc, pw = score_sb[r, :], pool_w[r, :]
                mx, sm, inv = (win_stat[r, i, :] for i in range(3))
                dve.wait_ge(s_tokb, 16)
                ts(sc, t[r, 0:TIME], tokb_sb[r, :], None, ALU.add).then_inc(is_freed("score", hf), 1)
                wait_freed(dve, "score", hf)
                v = sc.rearrange("p (w k) -> p w k", k=K)
                link(red(mx, v, AX, ALU.max))
                tt(v, v, bc(mx, K), ALU.subtract).then_inc(S["score_shift"], 1)
                dve.wait_ge(S["pool_exp"], hf + 1)
                v = pw.rearrange("p (w k) -> p w k", k=K)
                link(red(sm, v, AX, ALU.add))
                link(nc.vector.reciprocal(inv, sm))
                link(tt(v, v, bc(inv, K), ALU.mult))
                other = slice(64 - 64 * hf, 128 - 64 * hf)
                link(nc.vector.tensor_copy(pool_ws[r, hf, :], pw))
                tt(pool_ws[other, hf, :], pw, pool_ws[r, hf, :].bitcast(F32), ALU.subtract)\
                    .then_inc(S["pool_w_ready"], 1)

            def pool_sum(hf, i):
                n = 4 * hf + i
                t = wait_filled(dve, "wb", hf, i)
                j = NJ * hf + 4 * i
                pr = prod[:, n % 2, :]
                sent = [m for m in range(n - 1) if m % 4 in GPSIMD_SUMS[m // 4]]
                if sent:
                    dve.wait_ge(S["pooled_p"], len(sent))
                tt(pr, t[:, :], x_sb[:, j:j + 4, :].rearrange("p j t -> p (j t)"), ALU.mult)\
                    .then_inc(is_freed("wb", hf, i), 1)
                wait_freed(dve, "wb", hf, i)
                if hf and i == 0:
                    wait_filled(dve, "hT", 1)
                if i in GPSIMD_SUMS[hf]:
                    return
                red(pooledT[:, 4 * W * i:4 * W * (i + 1)], pr.rearrange("p (w k) -> p w k", k=K), AX, ALU.add)\
                    .then_inc(S["pooled"], 1)

            def layernorm(o, h, nt):
                sm, ss, v, y, t = (stat[:, i, 0:nt] for i in range(5))
                dev, sqd = ktmp[:, 0, 0:nt, :], ktmp[:, 1, 0:nt, :]
                link(red(sm, h, AX, ALU.add))
                link(stt(out=dev, in0=bc(sm, D), scalar=-1.0 / D, in1=h, op0=ALU.mult, op1=ALU.add))
                link(tt(sqd, dev, dev, ALU.mult))
                link(red(ss, sqd, AX, ALU.add))
                link(ts(v, ss, 1.0 / D, EPS_LN, ALU.mult, ALU.add))
                link(rsqrt(y, v, t))
                d2 = dev.unsqueeze(2).to_broadcast([P, nt, 2, D])
                y2 = y.unsqueeze(2).unsqueeze(3).to_broadcast([P, nt, 2, D])
                return tt(o, d2, y2, ALU.mult)

            def ln1(q, nq):
                for i in range(q, q + nq):
                    wait_freed(dve, "hT", i)
                if q == 2:
                    wait_filled(dve, "xT", 1)
                c = 4 * (q % 2)
                layernorm(ln_sb[:, c:c + 4 * nq, :, :], h_sb[:, 4 * q:4 * (q + nq), :], 4 * nq).then_inc(S["ln_ready"], nq)

            def xs_lo(q):
                t = wait_filled(dve, "xT", q)
                dve.wait_ge(S["xs_hi"], q + 1)
                o = xs[64:128, 512 * (q % 2):512 * (q % 2) + 512]
                tt(o, t[64:128, :], o.bitcast(F32), ALU.subtract).then_inc(is_freed("xT", q), 1)

            def keys(hf):
                dve.wait_ge(S["keys_rotated"], hf + 1)
                ss, v, y, t = (stat[:, i, 0:NT] for i in range(4))
                link(red(ss, key_tmp[:, :, :], AX, ALU.add))
                link(ts(v, ss, 1.0 / D, EPS_RMS, ALU.mult, ALU.add))
                link(rsqrt(y, v, t))
                a = ktmp[:, 0, :, :]
                link(tt(a, kv_sb[:, :, 0:D], bc(y, D), ALU.mult))
                if hf:
                    wait_filled(dve, "KT", 0)
                g = key_gain[:, :].unsqueeze(1).unsqueeze(1).to_broadcast([P, NT, 2, D])
                tt(kn[:, :, :, :], a.unsqueeze(2).to_broadcast([P, NT, 2, D]), g, ALU.mult)\
                    .then_inc(S["kn_ready"], 1)

            def ssq_out(hf):
                t = wait_filled(dve, "ss", hf)
                nc.vector.tensor_copy(ssq_sb[:, :], t[:, 0:256]).then_inc(is_freed("ss", hf), 1)

            def query_scales(hf):
                t = wait_filled(dve, "ssT", hf)
                v, y, tmp = (rq_stat[:, i, :] for i in range(3))
                tv = t[:, 0:256].rearrange("p (i c h) -> p c i h", i=2, c=4)[:, :, :, 0:H]
                ts(v.rearrange("p (c i h) -> p c i h", c=4, i=2), tv, 1.0 / D, EPS_RMS, ALU.mult, ALU.add)\
                    .then_inc(is_freed("ssT", hf), 1)
                wait_freed(dve, "ssT", hf)
                rsqrt(y, v, tmp).then_inc(S["scales"], 1)
                dve.wait_ge(S["scales"], hf + 1)
                if hf:
                    move_scales(nc.vector.tensor_copy, hf).then_inc(S["scales_moved"], 1)

            def mask(hf, T):
                n = NT * hf + T
                t = wait_filled(dve, "S", hf, T)
                dve.wait_ge(s_cst, 16)
                if n >= PROB_RING:
                    m = n - PROB_RING
                    wait_filled(dve, "PT", m // NT, m % NT)
                e16 = prob[:, n % PROB_RING, :, :, :, :].rearrange("p g j h s -> p (g j) h s")
                sv = t[:, :].rearrange("p (n x) -> p n x", x=P)[:, :, 0:2 * W].rearrange("p n (h s) -> p n h s", h=2)
                m = cst[:, C_MASK:C_SELC].unsqueeze(1).unsqueeze(1).to_broadcast([P, 8, 2, W])
                tt(e16, sv, m, ALU.add).then_inc(is_freed("S", hf, T), 1)
                wait_freed(dve, "S", hf, T)
                e = prob[:, n % PROB_RING, :, :, :, :].rearrange("p g j h s -> p (g j h) s")
                red(row_stat[:, n % PROB_RING, 0, :], e, AX, ALU.max).then_inc(S["masked"], 1)

            def sums(hf, T):
                n = NT * hf + T
                dve.wait_ge(S["prob_exp"], n + 1)
                e = prob[:, n % PROB_RING, :, :, :, :].rearrange("p g j h s -> p (g j h) s")
                link(red(row_stat[:, n % PROB_RING, 1, :], e, AX, ALU.add))
                nc.vector.reciprocal(row_stat[:, n % PROB_RING, 2, :], row_stat[:, n % PROB_RING, 1, :])\
                    .then_inc(S["prob_sums"], 1)

            def attn(hf, extra):
                for T in range(NT + 1):
                    if T < NT:
                        mask(hf, T)
                    if T >= 1:
                        sums(hf, T - 1)
                    for f in extra.get(T, []):
                        f()

            def ln2(s):
                t0, nt = SEG[s]
                for q in range(t0 // 4, (t0 + nt) // 4):
                    t = wait_filled(dve, "yT", q)
                    tv = t[:, 0:256].rearrange("p (i c m) -> p c i m", c=2, m=D)
                    h, h2 = (b[:, 4 * q:4 * q + 4, :].rearrange("p (c i) m -> p c i m", c=2) for b in (h_sb, h2_sb))
                    tt(h2, tv, h, ALU.add).then_inc(is_freed("yT", q), 1)
                    wait_freed(dve, "yT", q)
                h2 = h2_sb[:, t0:t0 + nt, :]
                wait_filled(dve, *(("x2T", 0) if s else ("xT", 3)))
                o = ln2_sb[:, t0 % NT:t0 % NT + nt, :, :]
                layernorm(o, h2, nt).then_inc(S["ln2_ready"], 1)
                dve.wait_ge(S["ln2_ready"], s + 1)
                link(tt(h2, h2, o[:, :, 0, :], ALU.add))

            def xs2_lo(s):
                t0, nt = SEG[s]
                t = wait_filled(dve, "x2T", s)
                dve.wait_ge(S["xs2_hi"], s + 1)
                o = xs2[64:128, P * (t0 % NT):P * (t0 % NT + nt)]
                tt(o, t[64:128, 0:P * nt], o.bitcast(F32), ALU.subtract).then_inc(is_freed("x2T", s), 1)

            def router(s):
                nt = SEG[s][1]
                t = wait_filled(dve, "lg", s)
                lg = t[:, 0:nt * E].rearrange("p (n e) -> p n e", e=E)
                m0 = r1[:, 0, 0:nt]
                link(red(m0, lg, AX, ALU.max))
                tt(rt[:, 0, 0:nt, :], lg, bc(m0, E), ALU.subtract).then_inc(is_freed("lg", s), 1)

            def top2(s):
                t0, nt = SEG[s]
                p_, e1, o1, p2, e2, o2, cc = (rt[:, i, 0:nt, :] for i in range(7))
                sm, m1, m2, x1, dn = (r1[:, i, 0:nt] for i in range(1, 6))
                idx = cst[:, C_IDX:C_ROW].unsqueeze(1).to_broadcast([P, nt, E])
                dve.wait_ge(S["gate_exp"], s + 1)
                red(sm, p_, AX, ALU.add)

                def largest(q, m, eq, o):
                    link(red(m, q, AX, ALU.max))
                    link(tt(eq, q, bc(m, E), ALU.is_equal))
                    link(tt(eq, eq, idx, ALU.mult))
                    link(red(x1, eq, AX, ALU.max))
                    link(tt(o, eq, bc(x1, E), ALU.is_equal))

                largest(p_, m1, e1, o1)
                link(stt(out=p2, in0=o1, scalar=-4.0, in1=p_, op0=ALU.mult, op1=ALU.add))
                largest(p2, m2, e2, o2)
                link(tt(cc, o1, o2, ALU.add))
                link(tt(cc, cc, p_, ALU.mult))
                link(tt(m1, m1, m2, ALU.add))
                link(stt(out=sm, in0=sm, scalar=1e-12, in1=m1, op0=ALU.mult, op1=ALU.max))
                link(nc.vector.reciprocal(dn, sm))
                link(tt(cc, cc, bc(dn, E), ALU.mult))
                g = gate[:, t0:t0 + nt, :]
                link(nc.vector.tensor_copy(g[:, :, 0:E], cc))
                tt(g[:, :, E:2 * E], cc, g[:, :, 0:E].bitcast(F32), ALU.subtract).then_inc(S["gate_ready"], 1)

            def gate_hidden(s, i):
                t0, nt = SEG[s]
                n = 8 // nt
                wait_freed(dve, "L1", s, i)
                t = wait_filled(dve, "cb", s, i)
                h = hidden(s)[:, n * i:n * (i + 1), :]
                tt(h, t[:, :].rearrange("p (a n) -> p a n", a=n), h, ALU.mult).then_inc(is_freed("cb", s, i), 1)

            def finish(s):
                t0, nt = SEG[s]
                t = wait_filled(dve, "zT", s)
                tv = t[:, 0:64 * nt].rearrange("p (i c m) -> p c i m", c=2, m=D)
                r = h2_sb[:, t0:t0 + nt, :].rearrange("p (c i) m -> p c i m", c=2)
                tt(r, tv, r, ALU.add).then_inc(is_freed("zT", s), 1)

            def blocks():
                pool_softmax(0)
                pool_sum(0, 0)
                pool_sum(0, 1)
                ln1(0, 1)
                pool_sum(0, 2)
                xs_lo(0)
                pool_sum(0, 3)
                ln1(1, 1)
                xs_lo(1)
                pool_softmax(1)
                pool_sum(1, 0)
                key_gains()
                keys(0)
                pool_sum(1, 1)
                pool_sum(1, 2)
                ssq_out(0)
                pool_sum(1, 3)
                query_scales(0)
                ln1(2, 1)
                attn(0, {0: [lambda: ln1(3, 1)], 2: [lambda: xs_lo(2)], 4: [lambda: xs_lo(3)]})
                keys(1)
                expert_selectors()
                ln2(0)
                xs2_lo(0)
                ssq_out(1)
                router(0)
                query_scales(1)
                top2(0)
                attn(1, {i + 1: [lambda i=i: gate_hidden(0, i)] for i in range(4)})
                ln2(1)
                xs2_lo(1)
                router(1)
                top2(1)
                ln2(2)
                xs2_lo(2)
                gate_hidden(1, 0)
                router(2)
                gate_hidden(1, 1)
                top2(2)
                finish(0)
                for i in range(2):
                    gate_hidden(2, i)
                finish(1)
                finish(2)

            blocks()

        @block.tensor
        def _(pe):
            mm, turn = nc.tensor.matmul, nc.tensor.transpose

            def claim(*key):
                r = region_of[key]
                if use_of[key] > 1:
                    pe.wait_ge(freed[r], use_of[key] - 1)
                return ps[r]

            def done(ins, *key):
                ins.then_inc(filled[region_of[key]], 1)

            def keep_busy(o, *key):
                for _ in range(FILLERS.get(key, 0)):
                    mm(o[0:64, 0:256], zeros[:, 0:64], zeros[:, :], start=True, stop=True)

            def score(hf):
                o = claim("score", hf)
                keep_busy(o, "score", hf)
                pe.wait_ge(s_tokw, 32)
                for g in range(2):
                    pe.wait_ge(s_x[hf][g], 16)
                    for jj in range(8):
                        i = mm(o[64 * hf + 32 * g:64 * hf + 32 * g + 32, 0:TIME], wz[:, 30 - 2 * jj:62 - 2 * jj],
                               x_sb[:, NJ * hf + 8 * g + jj, :], start=jj == 0, stop=jj == 7)
                done(i, "score", hf)

            def wb(hf, q):
                o = claim("wb", hf, q)
                keep_busy(o, "wb", hf, q)
                pe.wait_ge(S["row_selectors"], 1)
                pe.wait_ge(S["pool_w_ready"], hf + 1)
                for j in range(4):
                    jj = 4 * q + j
                    i = mm(o[:, TIME * j:TIME * (j + 1)], row_sel[:, 2 * jj:2 * jj + 2, :].rearrange("p a f -> p (a f)"),
                           pool_ws[:, hf, :], start=True, stop=True)
                done(i, "wb", hf, q)

            def hT(q):
                o = claim("hT", q)
                keep_busy(o, "hT", q)
                by_pool = sum(m % 4 in GPSIMD_SUMS[m // 4] for m in range(2 * q + 2))
                pe.wait_ge(S["pooled"], 2 * q + 2 - by_pool)
                if by_pool:
                    pe.wait_ge(S["pooled_p"], by_pool)
                pe.wait_ge(s_cst, 16)
                for j in range(2):
                    c = P * (2 * (q % 2) + j)
                    i = turn(o[:, P * j:P * j + P], pooledT[:, c:c + P], ident)
                done(i, "hT", q)

            def xT(q):
                o = claim("xT", q)
                keep_busy(o, "xT", q)
                pe.wait_ge(S["ln_ready"], q + 1)
                for T in range(4):
                    i = turn(o[:, P * T:P * T + P], ln_sb[:, 4 * (q % 2) + T, :, :].rearrange("p c d -> p (c d)"), ident)
                done(i, "xT", q)

            def kv(q):
                wait_freed(pe, "xT", q)
                pe.wait_ge(S["weights_ready"], 2)
                o = claim("kv", q)
                for T in range(4):
                    x_ = xs[:, 512 * (q % 2) + P * T:512 * (q % 2) + P * T + P]
                    for part in range(2):
                        i = mm(o[:, P * T:P * T + P], x_, wkvT[:, part, :], start=part == 0, stop=part == 1)
                done(i, "kv", q)

            def A(hf, c, q):
                o = claim("A", hf, c, q)
                keep_busy(o, "A", hf, c, q)
                pe.wait_ge(S["weights_ready"], 1)
                wait_freed(pe, "xT", 2 * hf + c)
                for a in range(2):
                    p = 2 * q + a
                    for part in range(2):
                        i = mm(o[:, 512 * a:512 * a + 512], wqT[:, part, P * p:P * p + P], xs[:, 512 * c:512 * c + 512],
                               start=part == 0, stop=part == 1)
                done(i, "A", hf, c, q)

            def KT(hf):
                pe.wait_ge(S["kn_ready"], hf + 1)
                o = claim("KT", hf)
                for T in range(NT):
                    i = turn(o[:, P * T:P * T + P], kn[:, T, :, :].rearrange("p c d -> p (c d)"), ident)
                done(i, "KT", hf)

            def square_sums(hf, p):
                pe.wait_ge(S["q_squared_p"], NPAIR * hf + p + 1)
                pe.wait_ge(S["q_squared"], NPAIR * hf + p + 1)
                o = claim("ss", hf) if p == 0 else ps[region_of["ss", hf]]
                for c in range(4):
                    i = mm(o[32 * c:32 * c + 32, 0:256], cst[:, C_ONES + 32 * p:C_ONES + 32 * p + 32],
                           sq_sb[:, p % SQ_RING, 256 * c:256 * c + 256], start=p == 0, stop=p == NPAIR - 1)
                if p < NPAIR - 1:
                    i.then_inc(S["squares_used"], 1)
                else:
                    done(i, "ss", hf)

            def ssT(hf):
                wait_freed(pe, "ss", hf)
                o = claim("ssT", hf)
                for j in range(2):
                    i = turn(o[:, P * j:P * j + P], ssq_sb[:, P * j:P * j + P], ident)
                done(i, "ssT", hf)

            def Dj(hf, k):
                pe.wait_ge(s_rot, 16)
                if k == 0:
                    wait_freed(pe, "A", hf, 1, 2)
                    wait_freed(pe, "A", hf, 1, 3)
                o = claim("D", hf, k)
                qv = q_sb[:, :, :].rearrange("p a (b t) -> p a b t", t=W)
                for t in range(4):
                    i = mm(o[:, 256 * t:256 * t + 256], rot_sb[:, 4 * k + t, :], qv[:, :, :, 4 * k + t],
                           start=True, stop=True)
                done(i, "D", hf, k)

            def Sj(hf, T):
                if T == 0:
                    wait_freed(pe, "D", hf, 6)
                    wait_freed(pe, "D", hf, 7)
                    wait_freed(pe, "KT", hf)
                o = claim("S", hf, T)
                for g in range(2):
                    for j4 in range(4):
                        b = 4 * T + j4
                        i = mm(o[:, 512 * g + P * j4:512 * g + P * j4 + P],
                               qr_sb[:, b, 4 * g:4 * g + 4, :].rearrange("p a t -> p (a t)"),
                               key_block[:, b:b + 2, :].rearrange("p b s -> p (b s)"), start=True, stop=True)
                done(i, "S", hf, T)

            def PT(hf, T):
                n = NT * hf + T
                o = claim("PT", hf, T)
                keep_busy(o, "PT", hf, T)
                pe.wait_ge(S["prob_ready"], n + 1)
                for g in range(2):
                    for r in range(2):
                        c = P * (2 * g + r)
                        i = turn(o[:, c:c + P], prob[:, n % PROB_RING, g, 2 * r:2 * r + 2, :, :].rearrange("p j h s -> p (j h s)"),
                                 ident)
                done(i, "PT", hf, T)

            def PV(hf, T):
                n = NT * hf + T
                wait_freed(pe, "PT", hf, T)
                pe.wait_ge(S["values_in"], 4 * (hf + 1))
                o = claim("PV", hf, T)
                for j4 in range(4):
                    i = mm(o[:, 256 * j4:256 * j4 + 256], value_block[:, 4 * T + j4, :],
                           probT[:, n % 2, j4 // 2, :, :].rearrange("p g n -> p (g n)"), start=True, stop=True)
                done(i, "PV", hf, T)

            def OP(q):
                wait_freed(pe, "PV", q // 2, 4 * (q % 2) + 3)
                pe.wait_ge(s_wo, 16)
                o = claim("OP", q)
                for a in range(NPAIR):
                    for c in range(2):
                        x0 = 512 * (q % 2) + 256 * c
                        i = mm(o[64 * c:64 * c + 64, 0:256], woT[:, a, :], o_sb[:, a, x0:x0 + 256],
                               start=a == 0, stop=a == NPAIR - 1)
                done(i, "OP", q)

            def turned(src, x0, n, src_key, *key):
                wait_freed(pe, *src_key)
                o = claim(*key)
                for j in range(n):
                    i = turn(o[:, P * j:P * j + P], src[:, x0 + P * j:x0 + P * j + P], ident)
                done(i, *key)

            def x2T(s):
                t0, nt = SEG[s]
                o = claim("x2T", s)
                keep_busy(o, "x2T", s)
                pe.wait_ge(S["ln2_ready"], s + 1)
                for T in range(nt):
                    i = turn(o[:, P * T:P * T + P], ln2_sb[:, t0 % NT + T, :, :].rearrange("p c d -> p (c d)"), ident)
                done(i, "x2T", s)

            def lg(s):
                t0, nt = SEG[s]
                wait_freed(pe, "x2T", s)
                o = claim("lg", s)
                for T in range(nt):
                    c = P * (t0 % NT + T)
                    for part in range(2):
                        i = mm(o[:, E * T:E * T + E], xs2[:, c:c + P], routerT[:, part, :],
                               start=part == 0, stop=part == 1)
                done(i, "lg", s)

            def cT(s):
                t0, nt = SEG[s]
                pe.wait_ge(S["gate_ready"], s + 1)
                o = claim("cT", s)
                for T in range(nt):
                    i = turn(o[0:2 * E, P * T:P * T + P], gate[:, t0 + T, :].bitcast(F32), ident)
                done(i, "cT", s)

            def L1(s, i):
                t0, nt = SEG[s]
                wait_freed(pe, "x2T", s)
                pe.wait_ge(S["weights_ready"], 4)
                o = claim("L1", s, i)
                for c in range(2):
                    pr, x0 = (i, 512 * c) if nt == 8 else (2 * i + c, P * (t0 % NT))
                    for part in range(2):
                        ins = mm(o[:, 512 * c:512 * c + 512], w1s[:, part, P * pr:P * pr + P],
                                 xs2[:, x0:x0 + 512], start=part == 0, stop=part == 1)
                done(ins, "L1", s, i)

            def cb(s, i):
                t0, nt = SEG[s]
                pe.wait_ge(S["expert_selectors"], 1)
                wait_freed(pe, "cT", s)
                o = claim("cb", s, i)
                for c in range(2):
                    pr, x0 = (i, 512 * c) if nt == 8 else (2 * i + c, gate_cols(s))
                    ins = mm(o[:, 512 * c:512 * c + 512], expert_sel[:, pr, :], gateT[:, x0:x0 + 512], start=True, stop=True)
                done(ins, "cb", s, i)

            def L2(s):
                pe.wait_ge(s_wff, 64)
                o = claim("L2", s)
                n = 64 * SEG[s][1]
                g0 = gate_cols(s)
                for c in range(2):
                    mm(o[64 * c:64 * c + 64, 0:n], b2_sb[:, :], gateT[:, g0 + n * c:g0 + n * (c + 1)].bitcast(F32),
                       start=True, stop=False)
                second_layer(o, s, 0)
                second_layer(o, s, 1)

            def L2_end(s):
                o = ps[region_of["L2", s]]
                second_layer(o, s, 2)
                done(second_layer(o, s, 3), "L2", s)

            def second_layer(o, s, pr):
                n = 64 * SEG[s][1]
                wait_freed(pe, "cb", s, pr * SEG[s][1] // 8)
                for c in range(2):
                    i = mm(o[64 * c:64 * c + 64, 0:n], w2_sb[:, pr, :], hidden(s)[:, pr, n * c:n * (c + 1)],
                           start=False, stop=pr == 3)
                return i

            run = {"score": score, "wb": wb, "hT": hT, "xT": xT, "kv": kv, "A": A,
                   "KT": KT, "ss": lambda hf: None, "squares": square_sums, "ssT": ssT, "D": Dj, "S": Sj, "PT": PT, "PV": PV, "OP": OP,
                   "yT": lambda q: turned(y_sb, 256 * (q % 2), 2, ("OP", q), "yT", q), "x2T": x2T, "lg": lg, "cT": cT, "L1": L1,
                   "cb": cb, "L2": L2, "L2_end": L2_end, "zT": lambda s: turned(z_sb, 256 * (s == 2), SEG[s][1] // 2, ("L2", s), "zT", s)}
            pe.wait_ge(S["zeros_ready"], 1)
            for key, _ in jobs:
                run[key[0]](*key[1:])


def kernel(**inputs):
    import concourse.bacc as bacc
    from concourse.bass_utils import run_bass_kernel_spmd

    nc = bacc.Bacc("TRN2", target_bir_lowering=False, num_devices=1)
    a = {name.removeprefix("L0_"): np.asarray(v) for name, v in inputs.items()}
    const, rot = shape_constants()
    arrays = {
        "x": a["x"], "tok_w_t": a["tok_w"].T, "tok_b": a["tok_b"], "wq_t": a["attn_wq"].T, "wkv_t": a["attn_wkv"].T,
        "wo_t": a["attn_wo"].reshape(D, NPAIR, P).transpose(2, 1, 0).reshape(P, NPAIR * D),
        "q_norm_w": a["attn_q_norm_w"], "k_norm_w": a["attn_k_norm_w"], "router_t": a["ffn_router_w"].T,
        "w1_t": a["ffn_w1"].transpose(1, 0, 2).reshape(D, E * D),
        "b1_t": a["ffn_b1"].reshape(E // 2, P).T, "w2": a["ffn_w2"], "b2": a["ffn_b2"], "const": const, "rot": rot}
    arrays = {name: np.ascontiguousarray(v) for name, v in arrays.items()}
    args = [nc.dram_tensor(name, v.shape, mybir.dt.from_np(v.dtype), kind="ExternalInput").ap()
            for name, v in arrays.items()]
    args.append(nc.dram_tensor("out", (P, HALVES * NT, F), F32, kind="ExternalOutput").ap())
    audio_tower(nc, *args)
    out = run_bass_kernel_spmd(nc, [arrays], core_ids=[0]).results[0]["out"]
    return np.ascontiguousarray(out.reshape(4, W, B // 8, 2, F).transpose(2, 0, 3, 1, 4)).reshape(B, W, F)
```
